# Optimizing a Trainium2 kernel written in Bass

```python
import numpy as np
import jax
import jax.numpy as jnp

def _softmax(x, axis=-1):
    return jax.nn.softmax(x, axis=axis)

def _gelu(x):
    return jax.nn.gelu(x, approximate=True)

def _silu(x):
    return jax.nn.silu(x)

def _sigmoid(x):
    return jax.nn.sigmoid(x)

def _layernorm(x, axis=-1, eps=1e-05):
    m = jnp.mean(x, axis=axis, keepdims=True)
    v = jnp.var(x, axis=axis, keepdims=True)
    return (x - m) / jnp.sqrt(v + eps)

def _scatter_add(tgt, idx, src, axis=0):
    return tgt.at[idx].add(src)

def _segment_sum(src, seg, n):
    return jax.ops.segment_sum(src, seg, n)
kernel_name = 'mk_adaln_d1_jaxref_r8_610ca8'

def setup_inputs(seed: int=0):
    np.random.seed(seed)
    _w = jnp.asarray

    def _L0_attn_setup():
        import jax, jax.numpy as jnp
        import numpy as np
        import math
        B, S, H = (1, 256, 512)
        NH, NKV, HD = (32, 8, 128)
        GS = 128
        WBITS = 4
        ZERO = float(2 ** (WBITS - 1))
        THETA = 10000.0

        def _dequant_matmul(x, qw, scales):
            w = (qw.astype(jnp.float32) - ZERO) * jnp.repeat(scales, GS, axis=0)
            return x @ w

        def _rope_tables(seq_len, dtype):
            inv_freq = 1.0 / THETA ** (jnp.arange(0, HD, 2, dtype=jnp.float32) / HD)
            freqs = jnp.arange(seq_len, dtype=jnp.float32)[:, None] * inv_freq
            emb = jnp.concatenate([freqs, freqs], axis=-1)
            return (jnp.cos(emb).astype(dtype), jnp.sin(emb).astype(dtype))

        def _rotate_half(x):
            x1, x2 = jnp.split(x, 2, axis=-1)
            return jnp.concatenate([-x2, x1], axis=-1)

        def _apply_rope(x, cos, sin):
            return x * cos[None, None] + _rotate_half(x) * sin[None, None]
        key = jax.random.key(seed)
        ks = jax.random.split(key, 9)
        small = lambda k, shp: jax.random.uniform(k, shp, jnp.float32) * 0.01 + 0.001
        return {'hidden_states': jax.random.normal(ks[0], (B, S, H), jnp.float32), 'scales_q': small(ks[1], (H // GS, NH * HD)), 'scales_k': small(ks[2], (H // GS, NKV * HD)), 'scales_v': small(ks[3], (H // GS, NKV * HD)), 'scales_o': small(ks[4], (NH * HD // GS, H)), 'qw_q': jax.random.randint(ks[5], (H, NH * HD), 0, 2 ** WBITS, jnp.int32), 'qw_k': jax.random.randint(ks[6], (H, NKV * HD), 0, 2 ** WBITS, jnp.int32), 'qw_v': jax.random.randint(ks[7], (H, NKV * HD), 0, 2 ** WBITS, jnp.int32), 'qw_o': jax.random.randint(ks[8], (NH * HD, H), 0, 2 ** WBITS, jnp.int32)}
    _L0_attn_in = _L0_attn_setup()

    def _L0_ffn_setup():
        import jax, jax.numpy as jnp
        import numpy as np
        HD, M = (512, 1792)
        key = jax.random.key(seed)
        k_x, k_g, k_u, k_d = jax.random.split(key, 4)
        scale = 1.0 / np.sqrt(HD)
        x = jax.random.normal(k_x, (4, 256, HD), dtype=jnp.float16)
        W_gate = jax.random.normal(k_g, (M, HD), dtype=jnp.float16) * jnp.float16(scale)
        W_up = jax.random.normal(k_u, (M, HD), dtype=jnp.float16) * jnp.float16(scale)
        W_down = jax.random.normal(k_d, (HD, M), dtype=jnp.float16) * jnp.float16(1.0 / np.sqrt(M))
        return {'x': x, 'W_gate': W_gate, 'W_up': W_up, 'W_down': W_down}
    _L0_ffn_in = _L0_ffn_setup()
    _L0_c = _w((lambda *s: np.random.randn(*s).astype(np.float32) * 0.05)(1, 512))
    _L0_wmod = _w((lambda *s: np.random.randn(*s).astype(np.float32) * 0.05)(512, 6 * 512) * 512 ** (-0.5))
    _d = {'L0_attn_hidden_states': _L0_attn_in['hidden_states'], 'L0_attn_scales_q': _L0_attn_in['scales_q'], 'L0_attn_scales_k': _L0_attn_in['scales_k'], 'L0_attn_scales_v': _L0_attn_in['scales_v'], 'L0_attn_scales_o': _L0_attn_in['scales_o'], 'L0_attn_qw_q': _L0_attn_in['qw_q'], 'L0_attn_qw_k': _L0_attn_in['qw_k'], 'L0_attn_qw_v': _L0_attn_in['qw_v'], 'L0_attn_qw_o': _L0_attn_in['qw_o'], 'L0_ffn_W_gate': _L0_ffn_in['W_gate'], 'L0_ffn_W_up': _L0_ffn_in['W_up'], 'L0_ffn_W_down': _L0_ffn_in['W_down'], 'L0_c': _L0_c, 'L0_wmod': _L0_wmod}
    _x0 = _d['L0_attn_hidden_states']
    _d['L0_attn_hidden_states'] = jax.random.normal(jax.random.fold_in(jax.random.key(seed), 1), (1, 1024, 512), dtype=_x0.dtype)
    del _x0
    return _d

def reference(L0_attn_hidden_states, L0_attn_scales_q, L0_attn_scales_k, L0_attn_scales_v, L0_attn_scales_o, L0_attn_qw_q, L0_attn_qw_k, L0_attn_qw_v, L0_attn_qw_o, L0_ffn_W_gate, L0_ffn_W_up, L0_ffn_W_down, L0_c, L0_wmod):

    def _L0_attn_ref(hidden_states, scales_q, scales_k, scales_v, scales_o, qw_q, qw_k, qw_v, qw_o):
        import jax, jax.numpy as jnp
        import numpy as np
        import math
        B, S, H = (1, 256, 512)
        NH, NKV, HD = (32, 8, 128)
        GS = 128
        WBITS = 4
        ZERO = float(2 ** (WBITS - 1))
        THETA = 10000.0

        def _dequant_matmul(x, qw, scales):
            w = (qw.astype(jnp.float32) - ZERO) * jnp.repeat(scales, GS, axis=0)
            return x @ w

        def _rope_tables(seq_len, dtype):
            inv_freq = 1.0 / THETA ** (jnp.arange(0, HD, 2, dtype=jnp.float32) / HD)
            freqs = jnp.arange(seq_len, dtype=jnp.float32)[:, None] * inv_freq
            emb = jnp.concatenate([freqs, freqs], axis=-1)
            return (jnp.cos(emb).astype(dtype), jnp.sin(emb).astype(dtype))

        def _rotate_half(x):
            x1, x2 = jnp.split(x, 2, axis=-1)
            return jnp.concatenate([-x2, x1], axis=-1)

        def _apply_rope(x, cos, sin):
            return x * cos[None, None] + _rotate_half(x) * sin[None, None]
        b, s, _ = hidden_states.shape
        q = _dequant_matmul(hidden_states, qw_q, scales_q).reshape(b, s, NH, HD).transpose(0, 2, 1, 3)
        k = _dequant_matmul(hidden_states, qw_k, scales_k).reshape(b, s, NKV, HD).transpose(0, 2, 1, 3)
        v = _dequant_matmul(hidden_states, qw_v, scales_v).reshape(b, s, NKV, HD).transpose(0, 2, 1, 3)
        cos, sin = _rope_tables(s, hidden_states.dtype)
        q = _apply_rope(q, cos, sin)
        k = _apply_rope(k, cos, sin)
        rep = NH // NKV
        k = jnp.repeat(k, rep, axis=1)
        v = jnp.repeat(v, rep, axis=1)
        scores = jnp.einsum('bhqd,bhkd->bhqk', q, k) / math.sqrt(HD)
        causal = jnp.tril(jnp.ones((s, s), dtype=bool))
        scores = jnp.where(causal[None, None], scores, jnp.finfo(scores.dtype).min)
        attn = jax.nn.softmax(scores.astype(jnp.float32), axis=-1).astype(q.dtype)
        ctx = jnp.einsum('bhqk,bhkd->bhqd', attn, v)
        ctx = ctx.transpose(0, 2, 1, 3).reshape(b, s, NH * HD)
        return _dequant_matmul(ctx, qw_o, scales_o)

    def _L0_ffn_ref(x, W_gate, W_up, W_down):
        import jax, jax.numpy as jnp
        import numpy as np
        HD, M = (512, 1792)
        gate = jnp.einsum('bsh,mh->bsm', x, W_gate)
        up = jnp.einsum('bsh,mh->bsm', x, W_up)
        h = jax.nn.silu(gate) * up
        out = jnp.einsum('bsm,hm->bsh', h, W_down)
        return out
    x = L0_attn_hidden_states
    mod = (_silu(L0_c) @ L0_wmod).reshape(L0_c.shape[0], 6, 1, -1)
    sa, ca, ga, sb, cb, gb = (mod[:, 0], mod[:, 1], mod[:, 2], mod[:, 3], mod[:, 4], mod[:, 5])
    ga = (2 * (ga >= 0) - 1) * jnp.maximum(jnp.abs(ga), 0.25)
    gb = (2 * (gb >= 0) - 1) * jnp.maximum(jnp.abs(gb), 0.25)
    h = _layernorm(x, axis=-1) * (1 + ca) + sa
    x = x + ga * _L0_attn_ref(h, L0_attn_scales_q, L0_attn_scales_k, L0_attn_scales_v, L0_attn_scales_o, L0_attn_qw_q, L0_attn_qw_k, L0_attn_qw_v, L0_attn_qw_o)
    h = _layernorm(x, axis=-1) * (1 + cb) + sb
    x = x + gb * _L0_ffn_ref(h, L0_ffn_W_gate, L0_ffn_W_up, L0_ffn_W_down)
    return x

_drawn_inputs = setup_inputs


def setup_inputs(seed=0):
    import zlib

    import numpy as np

    out = dict(_drawn_inputs(seed))
    spreads = {}
    factors = {'L0_attn_scales_q': 8.0,
     'L0_attn_scales_k': 8.0,
     'L0_attn_scales_v': 3.879,
     'L0_attn_scales_o': 4.09}
    for name, (base, spread) in spreads.items():
        noise = np.random.default_rng([zlib.crc32(name.encode()), seed]).standard_normal(out[name].shape)
        drawn = base * np.exp(spread * noise) if base else spread * noise
        out[name] = jnp.asarray(drawn.astype(out[name].dtype))
    for name, factor in factors.items():
        out[name] = (out[name] * factor).astype(out[name].dtype)
    return out
```

```python
from contextlib import ExitStack

import concourse.bass as bass
from concourse import mybir

ALU = mybir.AluOpType
ACT = mybir.ActivationFunctionType
AX = mybir.AxisListType
F32 = mybir.dt.float32
F32R = mybir.dt.float32r
BF16 = mybir.dt.bfloat16
F16 = mybir.dt.float16
I32 = mybir.dt.int32

P = 128
S, H = 1024, 512
NH, NKV, HD = 32, 8, 128
HPG = NH // NKV
M = 1792
KT = H // P
ST = S // P
QB = 512
NB = S // QB
TPB = QB // P
UNITS = NB * HPG
TILES = UNITS * TPB
JOBS = 2 + 2 * HPG
JWK, JWV, JWQ, JWO = 0, 1, 2, 2 + HPG
SCALE = float(HD) ** -0.5
EPS = 1e-5
ZERO = 8.0
MT = M // P
NSMALL = 256


def f32(ap):
    return ap.bitcast(F32)


class Allocator:
    def __init__(self, nc, ctx):
        self.nc, self.ctx = nc, ctx

    def sbuf(self, name, shape, dt=F32):
        return self.ctx.enter_context(self.nc.sbuf_tensor(name, shape, dt))

    def psum(self, name, shape, dt=F32):
        return self.ctx.enter_context(self.nc.psum_tensor(name, shape, dt))

    def sem(self, name):
        return self.ctx.enter_context(self.nc.semaphore(name))


def normalise_phase(nc, tag, x_dram, x_sb, wmod_dram, c_dram, ident, hT_hi, hT_lo):
    ctx = ExitStack()
    with ctx:
        al = Allocator(nc, ctx)
        sbuf, psum, sem = al.sbuf, al.psum, (lambda n: al.sem(tag + n))
        wmod = sbuf(tag + "wmod", [P, KT, 2 * H])
        c_col, c_silu = sbuf(tag + "c_col", [P, KT]), sbuf(tag + "c_silu", [P, KT])
        mod, scale1 = sbuf(tag + "mod", [P, 2 * KT]), sbuf(tag + "scale1", [P, KT])
        x = x_sb if x_sb is not None else sbuf(tag + "x", [P, ST, H])
        stats, mv = sbuf(tag + "stats", [P, ST, 6]), sbuf(tag + "mv", [P, ST, 2])
        std, rstd = sbuf(tag + "std", [P, ST]), sbuf(tag + "rstd", [P, ST])
        xn = sbuf(tag + "xn", [P, ST, H])
        z = sbuf(tag + "z", [P, 2, QB])
        ps_mod, ps_t = psum(tag + "ps_mod", [P, 512]), psum(tag + "ps_t", [P, 2, 512])
        mod_loaded, silu_done, mod_ready, mod_copied = (sem(n) for n in ("mod_loaded", "silu_done", "mod_ready",
                                                                         "mod_copied"))
        x_loaded = [sem(f"x_loaded{b}") for b in range(NB)]
        stats_done, aggr_done, var_done, std_done, rstd_done, xn_done = (
            sem(n) for n in ("stats_done", "aggr_done", "var_done", "std_done", "rstd_done", "xn_done"))
        turned, modulated, hi_done, lo_done = (sem(n) for n in ("turned", "modulated", "hi_done", "lo_done"))
        block = ctx.enter_context(nc.Block())

        @block.sync
        def _(sp):
            if x_sb is None:
                for b in range(NB):
                    sp.dma_start(x[:, b * TPB:(b + 1) * TPB, :],
                                 x_dram[b * QB:(b + 1) * QB, :].rearrange("(t p) n -> p t n", p=P))\
                        .then_inc(x_loaded[b], 16)

        @block.gpsimd
        def _(pool):
            pool.dma_start(c_col[:, :], c_dram).then_inc(mod_loaded, 16)
            pool.dma_start(wmod[:, :, :], wmod_dram.rearrange("(t p) n -> p t n", p=P)).then_inc(mod_loaded, 16)

        @block.vector
        def _(dve):
            for b in range(NB):
                tiles = range(b * TPB, (b + 1) * TPB)
                if x_sb is None:
                    dve.wait_ge(x_loaded[b], 16)
                for i in tiles:
                    dve.bn_stats(stats[:, i, :], x[:, i, :]).then_inc(stats_done, 1)
                for i in tiles:
                    dve.wait_ge(stats_done, i + 1)
                    dve.bn_aggr(mv[:, i, :], stats[:, i, :]).then_inc(aggr_done, 1)
                half = slice(b * TPB, (b + 1) * TPB)
                dve.wait_ge(aggr_done, (b + 1) * TPB)
                dve.tensor_scalar(std[:, half], mv[:, half, 1], EPS, None, ALU.add).then_inc(var_done, 1)
                dve.wait_ge(std_done, b + 1)
                dve.reciprocal(rstd[:, half], std[:, half]).then_inc(rstd_done, 1)
                dve.wait_ge(rstd_done, b + 1)
                for i in tiles:
                    dve.tensor_scalar(xn[:, i, :], x[:, i, :], mv[:, i, 0:1], rstd[:, i:i + 1],
                                      ALU.subtract, ALU.mult).then_inc(xn_done, 1)
            dve.wait_ge(mod_ready, 1)
            dve.tensor_copy(mod[:, :], ps_mod[:, 0:2 * KT]).then_inc(mod_copied, 1)
            dve.tensor_scalar(scale1[:, :], ps_mod[:, KT:2 * KT], 1.0, None, ALU.add).then_inc(mod_copied, 1)
            for n in range(NB * KT):
                b, kt = n // KT, n % KT
                c = slice(b * QB, (b + 1) * QB)
                dve.wait_ge(hi_done, n + 1)
                dve.tensor_tensor(hT_lo[:, kt, c], z[:, n % 2, :], f32(hT_hi[:, kt, c]),
                                  ALU.subtract).then_inc(lo_done, 1)

        @block.scalar
        def _(act):
            for b in range(NB):
                half = slice(b * TPB, (b + 1) * TPB)
                act.wait_ge(var_done, b + 1)
                act.activation(std[:, half], std[:, half], ACT.Sqrt).then_inc(std_done, 1)
            act.wait_ge(mod_loaded, 32)
            act.activation(c_silu[:, :], c_col[:, :], ACT.Silu).then_inc(silu_done, 1)
            act.wait_ge(mod_copied, 2)
            for n in range(NB * KT):
                b, kt = n // KT, n % KT
                act.wait_ge(turned, n + 1)
                if n >= 2:
                    act.wait_ge(lo_done, n - 1)
                act.activation(z[:, n % 2, :], ps_t[:, n % 2, :], ACT.Identity, bias=mod[:, kt:kt + 1],
                               scale=scale1[:, kt:kt + 1]).then_inc(modulated, 1)
                act.wait_ge(modulated, n + 1)
                act.copy(hT_hi[:, kt, b * QB:(b + 1) * QB], z[:, n % 2, :]).then_inc(hi_done, 1)

        @block.tensor
        def _(pe):
            pe.wait_ge(silu_done, 1)
            for j in range(2 * KT):
                for kt in range(KT):
                    mm = pe.matmul(ps_mod[:, j:j + 1], wmod[:, kt, j * P:(j + 1) * P], c_silu[:, kt:kt + 1],
                                   start=(kt == 0), stop=(kt == KT - 1))
            mm.then_inc(mod_ready, 1)
            for n in range(NB * KT):
                b, kt = n // KT, n % KT
                if kt == 0:
                    pe.wait_ge(xn_done, (b + 1) * TPB)
                if n >= 2:
                    pe.wait_ge(modulated, n - 1)
                for t in range(TPB):
                    mm = pe.transpose(ps_t[:, n % 2, t * P:(t + 1) * P], xn[:, b * TPB + t, kt * P:(kt + 1) * P],
                                      ident[:, :])
                mm.then_inc(turned, 1)


def chunks_of(n):
    b, t = n // (HPG * TPB), n % TPB
    first = n if b == 0 else HPG * TPB + 2 * (n - HPG * TPB)
    width = b * TPB + t + 1
    return [(first + k, TPB * k, min(TPB, width - TPB * k)) for k in range(b + 1)]


CHUNKS = HPG * TPB * 3


def attention_phase(nc, hT_hi, hT_lo, acc, ident, identb, maskb, wjobs, sjobs, cos_dram, sin_dram, r_scratch):
    ctx = ExitStack()
    with ctx:
        al = Allocator(nc, ctx)
        sbuf, psum, sem = al.sbuf, al.psum, al.sem

        cosT, sinT = sbuf("cosT", [P, S]), sbuf("sinT", [P, S])
        kT_hi, kT_lo = sbuf("kT_hi", [P, S], F32R), sbuf("kT_lo", [P, S], F32R)
        v_hi, v_lo = sbuf("v_hi", [P, ST, HD], F32R), sbuf("v_lo", [P, ST, HD], F32R)
        wk_hi, wk_lo = sbuf("wk_hi", [P, KT, HD], F32R), sbuf("wk_lo", [P, KT, HD], F32R)
        wv_hi, wv_lo = sbuf("wv_hi", [P, KT, HD], F32R), sbuf("wv_lo", [P, KT, HD], F32R)
        wq_hi = [sbuf(f"wq_hi{h}", [P, KT, HD], F32R) for h in range(HPG)]
        wq_lo = [sbuf(f"wq_lo{h}", [P, KT, HD], F32R) for h in range(HPG)]
        wo_hi = [sbuf(f"wo_hi{h}", [P, H], F32R) for h in range(HPG)]
        wo_lo = [sbuf(f"wo_lo{h}", [P, H], F32R) for h in range(HPG)]
        w_int, w_scale = sbuf("w_int", [P, 2, H], I32), sbuf("w_scale", [P, 2, H])
        w_full = sbuf("w_full", [P, 2, H])
        qT_hi, qT_lo = sbuf("qT_hi", [P, 2, QB], F32R), sbuf("qT_lo", [P, 2, QB], F32R)
        swapped, roped, sined = sbuf("swapped", [P, QB]), sbuf("roped", [P, QB]), sbuf("sined", [P, QB])
        probs = sbuf("probs", [P, 2, S])
        vT = probs[:, 0, :]
        pT_hi, pT_lo = sbuf("pT_hi", [P, ST, QB], F32R), sbuf("pT_lo", [P, ST, QB], F32R)
        ctx_hi, ctx_lo = sbuf("ctx_hi", [P, HPG, QB], F32R), sbuf("ctx_lo", [P, HPG, QB], F32R)
        ctx_full = sbuf("ctx_full", [P, QB])
        r_spread = sbuf("r_spread", [P, 2, QB])
        neg_max = sbuf("neg_max", [P, 2])
        row_sum = sbuf("row_sum", [P, 2, TPB])
        row_recip = sbuf("row_recip", [P, 2, TPB])

        ps = psum("ps", [P, 8, 512])
        SCORES = [ps[:, 0:2, :].rearrange("p a n -> p (a n)"), ps[:, 2:4, :].rearrange("p a n -> p (a n)")]
        TURN, CTX, PROJ = [ps[:, 4, :], ps[:, 5, :]], ps[:, 6, :], ps[:, 7, :]

        tables_loaded, zeroed = sem("tables_loaded"), sem("zeroed")
        w_loaded = [sem("w_loaded0"), sem("w_loaded1")]
        w_dequant, w_hi_done, w_lo_done = sem("w_dequant"), sem("w_hi_done"), sem("w_lo_done")
        k_proj, k_swapped, k_cos, k_sin, k_roped, k_hi_done, k_lo_done = (
            sem(n) for n in ("k_proj", "k_swapped", "k_cos", "k_sin", "k_roped", "k_hi_done", "k_lo_done"))
        v_proj, v_copied, v_turned, v_hi_done, v_lo_done = (
            sem(n) for n in ("v_proj", "v_copied", "v_turned", "v_hi_done", "v_lo_done"))
        q_proj, q_swapped, q_cos, q_sin, q_roped, q_hi_done, q_lo_done = (
            sem(n) for n in ("q_proj", "q_swapped", "q_cos", "q_sin", "q_roped", "q_hi_done", "q_lo_done"))
        scores_ready, max_ready, probs_ready = sem("scores_ready"), sem("max_ready"), sem("probs_ready")
        turn_ready, turn_hi, turn_lo = sem("turn_ready"), sem("turn_hi"), sem("turn_lo")
        recip_ready, r_stored, r_loaded = sem("recip_ready"), sem("r_stored"), sem("r_loaded")
        ctx_ready, ctx_scaled, ctx_hi_done, ctx_lo_done = (
            sem(n) for n in ("ctx_ready", "ctx_scaled", "ctx_hi_done", "ctx_lo_done"))
        out_ready, out_added = sem("out_ready"), sem("out_added")

        block = ctx.enter_context(nc.Block())

        def over_groups(eng, body, before=None):
            if before is not None:
                before()
            with eng.Fori(0, NKV - 1) as g:
                body(g, False)
            body(NKV - 1, True)

        def jobs_in(u, last):
            if u < HPG:
                return [(JWO + u, False)]
            todo = {HPG: [JWK, JWV], HPG + 1: [JWQ], HPG + 2: [JWQ + 1], HPG + 3: [JWQ + 2, JWQ + 3]}[u]
            return [] if last else [(k, True) for k in todo]

        def w_parts(k):
            if k == JWK:
                hi, lo = wk_hi, wk_lo
            elif k == JWV:
                hi, lo = wv_hi, wv_lo
            elif k < JWO:
                hi, lo = wq_hi[k - JWQ], wq_lo[k - JWQ]
            else:
                return wo_hi[k - JWO][:, :], wo_lo[k - JWO][:, :]
            return hi[:, :, :].rearrange("p t n -> p (t n)"), lo[:, :, :].rearrange("p t n -> p (t n)")

        @block.sync
        def _(sp):
            def load_job(g, k):
                slot = k % 2
                sp.dma_start(w_int[:, slot, :], wjobs[g, k]).then_inc(w_loaded[slot], 16)
                sp.dma_start(w_scale[:, slot, :], sjobs[g, k].partition_broadcast(P)).then_inc(w_loaded[slot], 16)

            def before():
                load_job(0, 0)
                load_job(0, 1)
                sp.dma_start(cosT[:, :], cos_dram).then_inc(tables_loaded, 16)
                sp.dma_start(sinT[:, :], sin_dram).then_inc(tables_loaded, 16)
                for k in range(2, JWO + 2):
                    sp.wait_ge(w_dequant, k - 1)
                    load_job(0, k)

            def spread_recip(g, u):
                sp.wait_ge(recip_ready, g * UNITS + u + 1)
                sp.dma_start(r_scratch[u % 2].rearrange("(t p) -> p t", p=P), row_recip[:, u % 2, :],
                             allow_slow_non_contiguous=True).then_inc(r_stored, 16)
                sp.wait_ge(r_stored, (g * UNITS + u + 1) * 16)
                sp.dma_start(r_spread[:, u % 2, :], r_scratch[u % 2].partition_broadcast(P)).then_inc(r_loaded, 16)

            def body(g, last):
                for u in range(UNITS):
                    if u:
                        spread_recip(g, u - 1)
                    for k, nxt in jobs_in(u, last):
                        ahead = k + 2 + JOBS * nxt
                        if last and ahead >= JOBS:
                            continue
                        sp.wait_ge(w_dequant, (g + nxt) * JOBS + k + 1)
                        load_job(g + ahead // JOBS, ahead % JOBS)
                spread_recip(g, UNITS - 1)
            over_groups(sp, body, before)

        @block.gpsimd
        def _(pool):
            pool.memset(f32(pT_hi[:, 5, 0:P]), 0.0)
            pool.memset(f32(pT_lo[:, 5, 0:P]), 0.0)
            pool.memset(f32(pT_hi[:, 7, 2 * P:3 * P]), 0.0)
            pool.memset(f32(pT_lo[:, 7, 2 * P:3 * P]), 0.0).then_inc(zeroed, 1)

        @block.scalar
        def _(act):
            def w_hi(count, k):
                act.wait_ge(w_dequant, count)
                act.copy(w_parts(k)[0], w_full[:, k % 2, :]).then_inc(w_hi_done, 1)

            def swap_halves(src):
                act.copy(swapped[0:64, :], src[64:128, :])
                return act.copy(swapped[64:128, :], src[0:64, :])

            def q_hi(g, u):
                act.wait_ge(q_roped, g * UNITS + u + 1)
                act.copy(qT_hi[:, u % 2, :], roped[:, :]).then_inc(q_hi_done, 1)

            def q_swap(g, u, src):
                act.wait_ge(q_proj, g * UNITS + u + 1)
                swap_halves(src).then_inc(q_swapped, 1)

            def turn(g, n):
                for c, j0, nj in chunks_of(n):
                    b, t = n // (HPG * TPB), n % TPB
                    j0 += TPB * (1 - b)
                    act.wait_ge(turn_ready, g * CHUNKS + c + 1)
                    act.copy(pT_hi[:, j0:j0 + nj, t * P:(t + 1) * P],
                             TURN[c % 2][:, 0:nj * P].rearrange("p (j q) -> p j q", q=P)).then_inc(turn_hi, 1)

            def ctx_part(g, u):
                act.wait_ge(ctx_scaled, g * UNITS + u + 1)
                act.copy(ctx_hi[:, u % HPG, :], ctx_full[:, :]).then_inc(ctx_hi_done, 1)

            def before():
                for k in range(JWO):
                    w_hi(k + 1, k)

            def body(g, last):
                for half in range(NB):
                    act.wait_ge(k_proj, g * NB + half + 1)
                    if half:
                        act.wait_ge(k_sin, g * NB + half)
                    swap_halves(TURN[half]).then_inc(k_swapped, 1)
                    act.wait_ge(v_proj, g * NB + half + 1)
                    act.copy(vT[:, half * QB:(half + 1) * QB], (CTX, PROJ)[half]).then_inc(v_copied, 1)
                    act.wait_ge(k_roped, g * NB + half + 1)
                    act.copy(kT_hi[:, half * QB:(half + 1) * QB], roped[:, :]).then_inc(k_hi_done, 1)
                q_swap(g, 0, SCORES[0][:, 0:QB])
                act.wait_ge(v_turned, g + 1)
                act.copy(v_hi[:, :, :].rearrange("p t d -> p (t d)"), SCORES[1]).then_inc(v_hi_done, 1)
                q_hi(g, 0)
                for n in range(TILES):
                    u, t = n // TPB, n % TPB
                    b = u // HPG
                    width = (b * TPB + t + 1) * P
                    jobs = jobs_in(u, last)
                    act.wait_ge(max_ready, g * TILES + n + 1)
                    act.activation(probs[:, n % 2, 0:width], SCORES[n % 2][:, 0:width], ACT.Exp,
                                   bias=neg_max[:, n % 2:n % 2 + 1], scale=-1.0,
                                   accum_out=row_sum[:, u % 2, t:t + 1]).then_inc(probs_ready, 1)
                    if n:
                        turn(g, n - 1)
                    if t == 1 and u + 1 < UNITS:
                        q_swap(g, u + 1, PROJ)
                    if t == 2 and u + 1 < UNITS:
                        q_hi(g, u + 1)
                    if t == 3 and u:
                        ctx_part(g, u - 1)
                    if 1 <= t <= len(jobs):
                        k, nxt = jobs[t - 1]
                        w_hi((g + nxt) * JOBS + k + 1, k)
                turn(g, TILES - 1)
                ctx_part(g, UNITS - 1)
            over_groups(act, body, before)

        @block.vector
        def _(dve):
            def dequant(g, k):
                slot = k % 2
                dve.wait_ge(w_loaded[slot], (g * (JOBS // 2) + k // 2 + 1) * 32)
                if not (isinstance(g, int) and g == 0 and k < 2):
                    dve.wait_ge(w_lo_done, g * JOBS + k - 1)
                dve.scalar_tensor_tensor(out=w_full[:, slot, :], in0=w_int[:, slot, :], scalar=-ZERO,
                                         in1=w_scale[:, slot, :], op0=ALU.add, op1=ALU.mult).then_inc(w_dequant, 1)

            def w_lo(count, k):
                hi, lo = w_parts(k)
                dve.wait_ge(w_hi_done, count)
                dve.tensor_tensor(lo, w_full[:, k % 2, :], f32(hi), ALU.subtract).then_inc(w_lo_done, 1)

            def rope(src, cols, factor, i, swap_done, cos_done, sin_done, rope_done, roped_read):
                c = slice(cols * QB, (cols + 1) * QB)
                dve.wait_ge(roped_read[0], roped_read[1])
                dve.wait_ge(swap_done, i)
                dve.scalar_tensor_tensor(out=roped[:, :], in0=src, scalar=factor, in1=cosT[:, c],
                                         op0=ALU.mult, op1=ALU.mult).then_inc(cos_done, 1)
                dve.scalar_tensor_tensor(out=sined[:, :], in0=swapped[:, :], scalar=factor, in1=sinT[:, c],
                                         op0=ALU.mult, op1=ALU.mult).then_inc(sin_done, 1)
                dve.wait_ge(sin_done, i)
                dve.wait_ge(cos_done, i)
                dve.tensor_tensor(roped[:, :], roped[:, :], sined[:, :], ALU.add).then_inc(rope_done, 1)

            def q_rope(g, u, src):
                dve.wait_ge(q_proj, g * UNITS + u + 1)
                done = (q_lo_done, g * UNITS + u) if u else (k_lo_done, (g + 1) * NB)
                rope(src, u // HPG, -SCALE, g * UNITS + u + 1, q_swapped, q_cos, q_sin, q_roped, done)

            def q_lo(g, u):
                dve.wait_ge(q_hi_done, g * UNITS + u + 1)
                dve.tensor_tensor(qT_lo[:, u % 2, :], roped[:, :], f32(qT_hi[:, u % 2, :]),
                                  ALU.subtract).then_inc(q_lo_done, 1)

            def turn(g, n):
                for c, j0, nj in chunks_of(n):
                    b, t = n // (HPG * TPB), n % TPB
                    j0 += TPB * (1 - b)
                    dve.wait_ge(turn_hi, g * CHUNKS + c + 1)
                    dve.tensor_tensor(pT_lo[:, j0:j0 + nj, t * P:(t + 1) * P],
                                      TURN[c % 2][:, 0:nj * P].rearrange("p (j q) -> p j q", q=P),
                                      f32(pT_hi[:, j0:j0 + nj, t * P:(t + 1) * P]), ALU.subtract)\
                        .then_inc(turn_lo, 1)

            def recip(g, u):
                dve.wait_ge(probs_ready, g * TILES + (u + 1) * TPB)
                dve.reciprocal(row_recip[:, u % 2, :], row_sum[:, u % 2, :]).then_inc(recip_ready, 1)

            def ctx_scale(g, u):
                dve.wait_ge(ctx_ready, g * UNITS + u + 1)
                dve.wait_ge(r_loaded, (g * UNITS + u + 1) * 16)
                dve.tensor_tensor(ctx_full[:, :], CTX, r_spread[:, u % 2, :], ALU.mult).then_inc(ctx_scaled, 1)

            def ctx_part(g, u):
                dve.wait_ge(ctx_hi_done, g * UNITS + u + 1)
                dve.tensor_tensor(ctx_lo[:, u % HPG, :], ctx_full[:, :], f32(ctx_hi[:, u % HPG, :]),
                                  ALU.subtract).then_inc(ctx_lo_done, 1)

            def out_add(g, i, src):
                dve.wait_ge(out_ready, g * ST + i + 1)
                dve.tensor_tensor(acc[:, i, :], src, acc[:, i, :], ALU.add).then_inc(out_added, 1)

            def before():
                dve.memset(acc[:, :, :], 0.0).then_inc(out_added, 1)
                dve.wait_ge(out_added, 1)
                dequant(0, 0)
                for k in range(JWO):
                    if k + 1 < JWO:
                        dequant(0, k + 1)
                    w_lo(k + 1, k)
                dve.wait_ge(tables_loaded, 32)

            def body(g, last):
                for half in range(NB):
                    dve.wait_ge(k_proj, g * NB + half + 1)
                    if half:
                        done = (k_lo_done, g * NB + half)
                    else:
                        done = (w_lo_done, g * JOBS + JWO)
                    rope(TURN[half], half, 1.0, g * NB + half + 1, k_swapped, k_cos, k_sin, k_roped, done)
                    dve.wait_ge(k_hi_done, g * NB + half + 1)
                    c = slice(half * QB, (half + 1) * QB)
                    dve.tensor_tensor(kT_lo[:, c], roped[:, :], f32(kT_hi[:, c]), ALU.subtract).then_inc(k_lo_done, 1)
                q_rope(g, 0, SCORES[0][:, 0:QB])
                dve.wait_ge(v_hi_done, g + 1)
                dve.tensor_tensor(v_lo[:, :, :].rearrange("p t d -> p (t d)"), SCORES[1],
                                  f32(v_hi[:, :, :].rearrange("p t d -> p (t d)")),
                                  ALU.subtract).then_inc(v_lo_done, 1)
                q_lo(g, 0)
                for n in range(TILES):
                    u, t = n // TPB, n % TPB
                    b = u // HPG
                    width = (b * TPB + t + 1) * P
                    jobs = jobs_in(u, last)
                    dve.wait_ge(scores_ready, g * TILES + n + 1)
                    dve.tensor_reduce(neg_max[:, n % 2:n % 2 + 1], SCORES[n % 2][:, 0:width], AX.X,
                                      ALU.min).then_inc(max_ready, 1)
                    if n:
                        turn(g, n - 1)
                    if t == 0 and u:
                        recip(g, u - 1)
                    if u == HPG + 1 and t == 0:
                        for i in range(TPB):
                            out_add(g, i, (CTX, PROJ)[i % 2])
                    if t == 1 and u + 1 < UNITS:
                        q_rope(g, u + 1, PROJ)
                    if t == 2 and u + 1 < UNITS:
                        q_lo(g, u + 1)
                    if t == 2 and u:
                        ctx_scale(g, u - 1)
                    if t == 3 and u:
                        ctx_part(g, u - 1)
                    if t < len(jobs):
                        dequant(g + jobs[t][1], jobs[t][0])
                    if 2 <= t < 2 + len(jobs):
                        k, nxt = jobs[t - 2]
                        w_lo((g + nxt) * JOBS + k + 1, k)
                turn(g, TILES - 1)
                recip(g, UNITS - 1)
                ctx_scale(g, UNITS - 1)
                ctx_part(g, UNITS - 1)
                for i in range(TPB):
                    out_add(g, TPB + i, ps[:, i, :])
            over_groups(dve, body, before)

        @block.tensor
        def _(pe):
            def projected(out, w_hi, w_lo, b):
                c = slice(b * QB, (b + 1) * QB)
                for kt in range(KT):
                    pe.matmul(out, w_hi[:, kt, :], hT_hi[:, kt, c], start=(kt == 0), stop=False)
                    pe.matmul(out, w_hi[:, kt, :], hT_lo[:, kt, c], start=False, stop=False)
                    mm = pe.matmul(out, w_lo[:, kt, :], hT_hi[:, kt, c], start=False, stop=(kt == KT - 1))
                return mm

            def project_q(g, u, out):
                h = u % HPG
                projected(out, wq_hi[h], wq_lo[h], u // HPG).then_inc(q_proj, 1)

            def scores(g, n):
                u, t = n // TPB, n % TPB
                i = (u // HPG) * TPB + t
                out = SCORES[n % 2]
                if t == 0:
                    pe.wait_ge(q_lo_done, g * UNITS + u + 1)
                if n == 0:
                    pe.wait_ge(k_lo_done, (g + 1) * NB)
                elif n == 1:
                    pe.wait_ge(v_lo_done, g + 1)
                else:
                    pe.wait_ge(probs_ready, g * TILES + n - 1)
                width = (i + 1) * P
                q = slice(t * P, (t + 1) * P)
                for c0 in range(0, width, 512):
                    c = slice(c0, c0 + max(NSMALL, min(512, width - c0)))
                    pe.matmul(out[:, c], qT_hi[:, u % 2, q], kT_hi[:, c], start=True, stop=False)
                    pe.matmul(out[:, c], qT_hi[:, u % 2, q], kT_lo[:, c], start=False, stop=False)
                    diagonal = c0 + 512 >= width
                    mm = pe.matmul(out[:, c], qT_lo[:, u % 2, q], kT_hi[:, c], start=False, stop=not diagonal)
                mm = pe.matmul(out[:, i * P:(i + 1) * P], identb[:, :], maskb[:, :], start=False, stop=True)
                mm.then_inc(scores_ready, 1)

            def turn(g, n):
                pe.wait_ge(probs_ready, g * TILES + n + 1)
                for c, j0, nj in chunks_of(n):
                    if c >= 2:
                        pe.wait_ge(turn_lo, g * CHUNKS + c - 1)
                    for j in range(nj):
                        mm = pe.transpose(TURN[c % 2][:, j * P:(j + 1) * P],
                                          probs[:, n % 2, (j0 + j) * P:(j0 + j + 1) * P], ident[:, :])
                    mm.then_inc(turn_ready, 1)

            def times_v(g, u, side):
                b = u // HPG
                last_chunk = chunks_of(u * TPB + 2 * side + 1)[-1][0]
                pe.wait_ge(turn_lo, g * CHUNKS + last_chunk + 1)
                if side == 0 and u:
                    pe.wait_ge(ctx_scaled, g * UNITS + u)
                c = slice(side * 2 * P, (side + 1) * 2 * P)
                tiles = b * TPB + 2 * side + 2
                for j in range(tiles):
                    at = j + TPB * (1 - b)
                    pe.matmul(CTX[:, c], v_hi[:, j, :], pT_hi[:, at, c], start=(j == 0), stop=False)
                    pe.matmul(CTX[:, c], v_hi[:, j, :], pT_lo[:, at, c], start=False, stop=False)
                    mm = pe.matmul(CTX[:, c], v_lo[:, j, :], pT_hi[:, at, c], start=False, stop=(j == tiles - 1))
                if side == 1:
                    mm.then_inc(ctx_ready, 1)

            def project_out(tt, out):
                q = slice(tt * P, (tt + 1) * P)
                for h in range(HPG):
                    pe.matmul(out, ctx_hi[:, h, q], wo_hi[h][:, :], start=(h == 0), stop=False)
                    pe.matmul(out, ctx_hi[:, h, q], wo_lo[h][:, :], start=False, stop=False)
                    mm = pe.matmul(out, ctx_lo[:, h, q], wo_hi[h][:, :], start=False, stop=(h == HPG - 1))
                mm.then_inc(out_ready, 1)

            def body(g, last):
                pe.wait_ge(w_lo_done, g * JOBS + JWO)
                for half in range(NB):
                    projected(TURN[half], wk_hi, wk_lo, half).then_inc(k_proj, 1)
                for half in range(NB):
                    projected((CTX, PROJ)[half], wv_hi, wv_lo, half).then_inc(v_proj, 1)
                pe.wait_ge(out_added, g * ST + 1)
                project_q(g, 0, SCORES[0][:, 0:QB])
                pe.wait_ge(v_copied, (g + 1) * NB)
                for j in range(ST):
                    mm = pe.transpose(SCORES[1][:, j * P:(j + 1) * P], vT[:, j * P:(j + 1) * P], ident[:, :])
                mm.then_inc(v_turned, 1)
                scores(g, 0)
                for n in range(TILES):
                    u, t = n // TPB, n % TPB
                    if n + 1 < TILES:
                        scores(g, n + 1)
                    if u == HPG and t == 3:
                        pe.wait_ge(ctx_lo_done, g * UNITS + HPG)
                        project_out(0, CTX)
                        project_out(1, PROJ)
                    if u == HPG + 1 and t == 0:
                        pe.wait_ge(out_added, g * ST + 2)
                        project_out(2, CTX)
                        pe.wait_ge(out_added, g * ST + 3)
                        project_out(3, PROJ)
                    if t == 0 and u + 1 < UNITS:
                        if u == HPG + 1:
                            pe.wait_ge(out_added, g * ST + 1 + TPB)
                        project_q(g, u + 1, PROJ)
                    if u and t < 2:
                        times_v(g, u - 1, t)
                    turn(g, n)
                times_v(g, UNITS - 1, 0)
                times_v(g, UNITS - 1, 1)
                pe.wait_ge(ctx_lo_done, (g + 1) * UNITS)
                for i in range(TPB):
                    project_out(i, ps[:, i, :])

            pe.wait_ge(zeroed, 1)
            over_groups(pe, body)


def residual_phase(nc, tag, acc, gate, x_dram):
    ctx = ExitStack()
    with ctx:
        al = Allocator(nc, ctx)
        xin = al.sbuf(tag + "xin", [P, ST, H])
        x_loaded, scaled, added = al.sem(tag + "x_loaded"), al.sem(tag + "scaled"), al.sem(tag + "added")
        block = ctx.enter_context(nc.Block())

        @block.sync
        def _(sp):
            sp.dma_start(xin[:, :, :], x_dram.rearrange("(t p) n -> p t n", p=P)).then_inc(x_loaded, 16)

        @block.vector
        def _(dve):
            for i in range(ST):
                dve.tensor_tensor(acc[:, i, :], acc[:, i, :], gate, ALU.mult).then_inc(scaled, 1)
                if i == 0:
                    dve.wait_ge(x_loaded, 16)
                dve.wait_ge(scaled, i + 1)
                dve.tensor_tensor(acc[:, i, :], acc[:, i, :], xin[:, i, :], ALU.add).then_inc(added, 1)
            dve.wait_ge(added, ST)


def gate_phase(nc, gates, wga_dram, wgb_dram, c_dram):
    ctx = ExitStack()
    with ctx:
        al = Allocator(nc, ctx)
        wgate = al.sbuf("g_w", [P, KT, 2 * H])
        c_col, c_silu = al.sbuf("g_c", [P, KT]), al.sbuf("g_silu", [P, KT])
        sign, mag = al.sbuf("g_sign", [P, 2, H]), al.sbuf("g_mag", [P, 2, H])
        ps_g = al.psum("g_ps", [P, 2, 512])
        loaded, silu_done, ready, step = (al.sem("g_" + n) for n in ("loaded", "silu_done", "ready", "step"))
        block = ctx.enter_context(nc.Block())

        @block.sync
        def _(sp):
            sp.dma_start(c_col[:, :], c_dram).then_inc(loaded, 16)
            for i, w in enumerate((wga_dram, wgb_dram)):
                sp.dma_start(wgate[:, :, i * H:(i + 1) * H], w.rearrange("(t p) n -> p t n", p=P)).then_inc(loaded, 16)

        @block.scalar
        def _(act):
            act.wait_ge(loaded, 48)
            act.activation(c_silu[:, :], c_col[:, :], ACT.Silu).then_inc(silu_done, 1)

        @block.tensor
        def _(pe):
            pe.wait_ge(silu_done, 1)
            for i in range(2):
                for kt in range(KT):
                    mm = pe.matmul(ps_g[:, i, :], c_silu[:, kt:kt + 1].to_broadcast([P, P]),
                                   wgate[:, kt, i * H:(i + 1) * H], start=(kt == 0), stop=(kt == KT - 1))
            mm.then_inc(ready, 1)

        @block.vector
        def _(dve):
            dve.wait_ge(ready, 1)
            dve.tensor_scalar(sign[:, :, :], ps_g[:, :, :], 0.0, 2.0, ALU.is_ge, ALU.mult).then_inc(step, 1)
            dve.tensor_scalar(mag[:, :, :], ps_g[:, :, :], -1.0, None, ALU.mult).then_inc(step, 1)
            dve.wait_ge(step, 2)
            dve.tensor_tensor(mag[:, :, :], mag[:, :, :], ps_g[:, :, :], ALU.max).then_inc(step, 1)
            dve.wait_ge(step, 3)
            dve.tensor_scalar(mag[:, :, :], mag[:, :, :], 0.25, None, ALU.max).then_inc(step, 1)
            dve.wait_ge(step, 4)
            dve.scalar_tensor_tensor(out=gates[:, :, :], in0=sign[:, :, :], scalar=-1.0, in1=mag[:, :, :],
                                     op0=ALU.add, op1=ALU.mult).then_inc(step, 1)
            dve.wait_ge(step, 5)


def ffn_phase(nc, hT_hi, hT_lo, x, gate, ffn_dram, out_dram):
    ctx = ExitStack()
    with ctx:
        al = Allocator(nc, ctx)
        sbuf, psum, sem = al.sbuf, al.psum, (lambda n: al.sem("ffn_" + n))
        raw = sbuf("ffn_raw", [P, 2, 3 * H], F16)
        w_gu = [sbuf(f"ffn_w_gu{s}", [P, 2 * KT, P], F32R) for s in range(2)]
        w_down = [sbuf(f"ffn_w_down{s}", [P, H], F32R) for s in range(2)]
        gated, mid = sbuf("ffn_gated", [P, 2, QB]), sbuf("ffn_mid", [P, 2, QB])
        mid_hi = [sbuf(f"ffn_mid_hi{s}", [P, QB], F32R) for s in range(2)]
        mid_lo = [sbuf(f"ffn_mid_lo{s}", [P, QB], F32R) for s in range(2)]
        fin = sbuf("ffn_fin", [P, TPB, H])
        ps = psum("ffn_ps", [P, 8, 512])
        loaded = [sem("loaded0"), sem("loaded1")]
        gu_cast, down_cast, gate_up, silued, product, hi_done, lo_done, down = (
            sem(n) for n in ("gu_cast", "down_cast", "gate_up", "silued", "product", "hi_done", "lo_done", "down"))
        scaled, added, stored = sem("scaled"), sem("added"), sem("stored")
        block = ctx.enter_context(nc.Block())
        PAIRS = MT // 2

        def over_steps(eng, body, first=0, after=None):
            for b in range(NB):
                for i in range(first):
                    for s in range(2):
                        body(b, i, s)
                with eng.Fori(first, PAIRS - 1) as i:
                    for s in range(2):
                        body(b, i, s)
                for s in range(2):
                    body(b, PAIRS - 1, s)
                if after is not None:
                    after(b)

        @block.sync
        def _(sp):
            for s in range(2):
                sp.dma_start(raw[:, s, :], ffn_dram[s]).then_inc(loaded[s], 16)

            def body(b, i, s):
                if isinstance(i, int):
                    if b == NB - 1:
                        return
                    i_next = 0
                else:
                    i_next = i + 1
                sp.wait_ge(down_cast, b * MT + i * 2 + s + 1)
                sp.dma_start(raw[:, s, :], ffn_dram[i_next * 2 + s]).then_inc(loaded[s], 16)
            over_steps(sp, body)
            for b in range(NB):
                sp.wait_ge(added, (b + 1) * TPB)
                sp.dma_start(out_dram[b * QB:(b + 1) * QB, :].rearrange("(t p) n -> p t n", p=P),
                             x[:, b * TPB:(b + 1) * TPB, :]).then_inc(stored, 16)
            sp.wait_ge(stored, 16 * NB)

        @block.scalar
        def _(act):
            def body(b, i, s):
                m = b * MT + i * 2 + s
                act.wait_ge(gate_up, m + 1)
                act.activation(gated[:, s, :], ps[:, 2 * s, :], ACT.Silu).then_inc(silued, 1)
                act.wait_ge(product, m + 1)
                act.copy(mid_hi[s][:, :], mid[:, s, :]).then_inc(hi_done, 1)
            over_steps(act, body)

        @block.vector
        def _(dve):
            def cast_gu(count, s):
                dve.wait_ge(loaded[s], count * 16)
                dve.tensor_copy(w_gu[s][:, :, :].rearrange("p a n -> p (a n)"), raw[:, s, 0:2 * H]).then_inc(gu_cast, 1)

            def cast_down(s):
                dve.tensor_copy(w_down[s][:, :], raw[:, s, 2 * H:3 * H]).then_inc(down_cast, 1)

            def body(b, i, s):
                m = b * MT + i * 2 + s
                end = isinstance(i, int) and i == PAIRS - 1 and b == NB - 1
                dve.wait_ge(silued, m + 1)
                dve.tensor_tensor(mid[:, s, :], gated[:, s, :], ps[:, 2 * s + 1, :], ALU.mult).then_inc(product, 1)
                if not end:
                    cast_gu(b * PAIRS + i + 2, s)
                if not (end and s == 1):
                    if not (isinstance(m, int) and m == 0):
                        dve.wait_ge(down, m)
                    cast_down(1 - s)
                dve.wait_ge(hi_done, m + 1)
                dve.tensor_tensor(mid_lo[s][:, :], mid[:, s, :], f32(mid_hi[s][:, :]), ALU.subtract).then_inc(lo_done, 1)

            def after(b):
                dve.wait_ge(down, (b + 1) * MT)
                for t in range(TPB):
                    i = b * TPB + t
                    dve.tensor_tensor(fin[:, t, :], ps[:, 4 + t, :], gate, ALU.mult).then_inc(scaled, 1)
                    dve.wait_ge(scaled, i + 1)
                    dve.tensor_tensor(x[:, i, :], x[:, i, :], fin[:, t, :], ALU.add).then_inc(added, 1)

            cast_gu(1, 0)
            cast_gu(1, 1)
            cast_down(0)
            over_steps(dve, body, first=1, after=after)

        @block.tensor
        def _(pe):
            def project(b, i, s):
                m = b * MT + i * 2 + s
                pe.wait_ge(gu_cast, m + 1)
                if not (isinstance(i, int) and i == 0 and b == 0):
                    pe.wait_ge(product, m - 1)
                c = slice(b * QB, (b + 1) * QB)
                for a in range(2):
                    for kt in range(KT):
                        pe.matmul(ps[:, 2 * s + a, :], w_gu[s][:, a * KT + kt, :], hT_hi[:, kt, c],
                                  start=(kt == 0), stop=False)
                        mm = pe.matmul(ps[:, 2 * s + a, :], w_gu[s][:, a * KT + kt, :], hT_lo[:, kt, c],
                                       start=False, stop=(kt == KT - 1))
                mm.then_inc(gate_up, 1)

            def project_down(m, s, first=False, last=False):
                pe.wait_ge(lo_done, m + 1)
                for t in range(TPB):
                    q = slice(t * P, (t + 1) * P)
                    pe.matmul(ps[:, 4 + t, :], mid_hi[s][:, q], w_down[s][:, :], start=first, stop=False)
                    mm = pe.matmul(ps[:, 4 + t, :], mid_lo[s][:, q], w_down[s][:, :], start=False, stop=last)
                mm.then_inc(down, 1)

            def body(b, i, s):
                project(b, i, s)
                m = b * MT + i * 2 + s
                if isinstance(i, int) and i == 0 and s == 0:
                    return
                first = isinstance(i, int) and i == 0
                if first and b:
                    pe.wait_ge(added, b * TPB)
                project_down(m - 1, 1 - s, first=first)

            def after(b):
                project_down((b + 1) * MT - 1, 1, last=True)
            over_steps(pe, body, first=1, after=after)


def build(nc, x, wmod, c, wjobs, sjobs, ffn, cos, sin, ident_dram, masks_dram, r_scratch, out):
    ctx = ExitStack()
    with ctx:
        al = Allocator(nc, ctx)
        hT_hi, hT_lo = al.sbuf("hT_hi", [P, KT, S], F32R), al.sbuf("hT_lo", [P, KT, S], F32R)
        acc = al.sbuf("acc", [P, ST, H])
        ident = al.sbuf("ident", [P, P])
        masks = al.sbuf("masks", [P, 2, P], BF16)
        consts_loaded = al.sem("consts_loaded")
        with nc.Block() as block:
            @block.sync
            def _(sp):
                sp.dma_start(ident[:, :], ident_dram).then_inc(consts_loaded, 16)
                sp.dma_start(masks[:, :, :], masks_dram).then_inc(consts_loaded, 16)
                sp.wait_ge(consts_loaded, 32)
        normalise_phase(nc, "n1_", x, None, wmod[:, 0:2 * H], c, ident, hT_hi, hT_lo)
        attention_phase(nc, hT_hi, hT_lo, acc, ident, masks[:, 0, :], masks[:, 1, :], wjobs, sjobs, cos, sin, r_scratch)
        gates = al.sbuf("gates", [P, 2, H])
        gate_phase(nc, gates, wmod[:, 2 * H:3 * H], wmod[:, 5 * H:6 * H], c)
        residual_phase(nc, "r1_", acc, gates[:, 0, :], x)
        normalise_phase(nc, "n2_", None, acc, wmod[:, 3 * H:5 * H], c, ident, hT_hi, hT_lo)
        ffn_phase(nc, hT_hi, hT_lo, acc, gates[:, 1, :], ffn, out)


def kernel(L0_attn_hidden_states, L0_attn_scales_q, L0_attn_scales_k, L0_attn_scales_v, L0_attn_scales_o,
           L0_attn_qw_q, L0_attn_qw_k, L0_attn_qw_v, L0_attn_qw_o, L0_ffn_W_gate, L0_ffn_W_up, L0_ffn_W_down,
           L0_c, L0_wmod):
    import numpy as np
    import concourse.bacc as bacc
    from concourse.bass_utils import run_bass_kernel_spmd

    def by_head(w, heads):
        return w.reshape(-1, P, heads, HD).transpose(2, 1, 0, 3).reshape(heads, P, -1)

    def scale_by_head(s, heads):
        return s.reshape(KT, heads, HD).transpose(1, 0, 2).reshape(heads, H)

    def jobs(k, v, q, o):
        return np.ascontiguousarray(np.concatenate(
            [k[:, None], v[:, None], q.reshape(NKV, HPG, *q.shape[1:]), o.reshape(NKV, HPG, *o.shape[1:])], axis=1))

    def array(a):
        return np.asarray(a)

    wjobs = jobs(by_head(array(L0_attn_qw_k), NKV), by_head(array(L0_attn_qw_v), NKV),
                 by_head(array(L0_attn_qw_q), NH), array(L0_attn_qw_o).reshape(NH, HD, H))
    sjobs = jobs(scale_by_head(array(L0_attn_scales_k), NKV), scale_by_head(array(L0_attn_scales_v), NKV),
                 scale_by_head(array(L0_attn_scales_q), NH), array(L0_attn_scales_o))

    def ffn_side(w):
        return w.reshape(MT, P, KT, P).transpose(0, 3, 2, 1).reshape(MT, P, H)

    ffn = np.ascontiguousarray(np.concatenate(
        [ffn_side(array(L0_ffn_W_gate)), ffn_side(array(L0_ffn_W_up)),
         array(L0_ffn_W_down).T.reshape(MT, P, H)], axis=2))

    inv_freq = (np.float32(1.0) / np.float32(10000.0) ** (np.arange(0, HD, 2, dtype=np.float32) / np.float32(HD)))
    angle = np.arange(S, dtype=np.float32)[:, None] * inv_freq.astype(np.float32)
    cos = np.ascontiguousarray(np.concatenate([np.cos(angle), np.cos(angle)], axis=1).T.astype(np.float32))
    sin = np.ascontiguousarray(np.concatenate([-np.sin(angle), np.sin(angle)], axis=1).T.astype(np.float32))
    bf16 = mybir.dt.np(BF16)
    masks = np.zeros((P, 2, P), bf16)
    masks[:, 0] = np.eye(P)
    masks[:, 1] = np.triu(np.full((P, P), 1e37), 1)

    arrays = {"x": array(L0_attn_hidden_states)[0], "wmod": array(L0_wmod), "c": np.ascontiguousarray(array(L0_c).reshape(KT, P).T), "wjobs": wjobs,
              "sjobs": sjobs, "ffn": ffn, "cos": cos, "sin": sin, "ident": np.eye(P, dtype=np.float32), "masks": masks}
    nc = bacc.Bacc("TRN2", target_bir_lowering=False, num_devices=1)
    aps = {n: nc.dram_tensor("in_" + n, a.shape, mybir.dt.from_np(a.dtype), kind="ExternalInput").ap()
           for n, a in arrays.items()}
    r_scratch = nc.dram_tensor("r_scratch", (2, QB), F32, kind="Internal").ap()
    out = nc.dram_tensor("out", (S, H), F32, kind="ExternalOutput").ap()
    build(nc, aps["x"], aps["wmod"], aps["c"], aps["wjobs"], aps["sjobs"], aps["ffn"], aps["cos"], aps["sin"],
          aps["ident"], aps["masks"], r_scratch, out)
    r = run_bass_kernel_spmd(nc, [{"in_" + n: a for n, a in arrays.items()}], core_ids=[0])
    return r.results[0]["out"].reshape(1, S, H)
```

```python
from contextlib import ExitStack

import concourse.bass as bass
from concourse import mybir

ALU = mybir.AluOpType
ACT = mybir.ActivationFunctionType
AX = mybir.AxisListType
F32 = mybir.dt.float32
F32R = mybir.dt.float32r
BF16 = mybir.dt.bfloat16
F16 = mybir.dt.float16
I32 = mybir.dt.int32

P = 128
S, H = 1024, 512
NH, NKV, HD = 32, 8, 128
HPG = NH // NKV
M = 1792
KT = H // P
ST = S // P
QB = 512
NB = S // QB
TPB = QB // P
UNITS = NB * HPG
TILES = UNITS * TPB
JOBS = 2 + 2 * HPG
JWK, JWV, JWQ, JWO = 0, 1, 2, 2 + HPG
SCALE = float(HD) ** -0.5
EPS = 1e-5
ZERO = 8.0
MT = M // P
NSMALL = 256


def f32(ap):
    return ap.bitcast(F32)


class Allocator:
    def __init__(self, nc, ctx):
        self.nc, self.ctx = nc, ctx

    def sbuf(self, name, shape, dt=F32):
        return self.ctx.enter_context(self.nc.sbuf_tensor(name, shape, dt))

    def psum(self, name, shape, dt=F32):
        return self.ctx.enter_context(self.nc.psum_tensor(name, shape, dt))

    def sem(self, name):
        return self.ctx.enter_context(self.nc.semaphore(name))


def normalise_phase(nc, tag, x_dram, x_sb, wmod_dram, c_dram, ident, hT_hi, hT_lo):
    ctx = ExitStack()
    with ctx:
        al = Allocator(nc, ctx)
        sbuf, psum, sem = al.sbuf, al.psum, (lambda n: al.sem(tag + n))
        wmod = sbuf(tag + "wmod", [P, KT, 2 * H])
        c_col, c_silu = sbuf(tag + "c_col", [P, KT]), sbuf(tag + "c_silu", [P, KT])
        mod, scale1 = sbuf(tag + "mod", [P, 2 * KT]), sbuf(tag + "scale1", [P, KT])
        x = x_sb if x_sb is not None else sbuf(tag + "x", [P, ST, H])
        stats, mv = sbuf(tag + "stats", [P, ST, 6]), sbuf(tag + "mv", [P, ST, 2])
        std, rstd = sbuf(tag + "std", [P, ST]), sbuf(tag + "rstd", [P, ST])
        xn = sbuf(tag + "xn", [P, ST, H])
        z = sbuf(tag + "z", [P, 2, QB])
        ps_mod, ps_t = psum(tag + "ps_mod", [P, 512]), psum(tag + "ps_t", [P, 2, 512])
        mod_loaded, silu_done, mod_ready, mod_copied = (sem(n) for n in ("mod_loaded", "silu_done", "mod_ready",
                                                                         "mod_copied"))
        x_loaded = [sem(f"x_loaded{b}") for b in range(NB)]
        stats_done, aggr_done, var_done, std_done, rstd_done, xn_done = (
            sem(n) for n in ("stats_done", "aggr_done", "var_done", "std_done", "rstd_done", "xn_done"))
        turned, modulated, hi_done, lo_done = (sem(n) for n in ("turned", "modulated", "hi_done", "lo_done"))
        block = ctx.enter_context(nc.Block())

        @block.sync
        def _(sp):
            if x_sb is None:
                for b in range(NB):
                    sp.dma_start(x[:, b * TPB:(b + 1) * TPB, :],
                                 x_dram[b * QB:(b + 1) * QB, :].rearrange("(t p) n -> p t n", p=P))\
                        .then_inc(x_loaded[b], 16)

        @block.gpsimd
        def _(pool):
            pool.dma_start(c_col[:, :], c_dram).then_inc(mod_loaded, 16)
            pool.dma_start(wmod[:, :, :], wmod_dram.rearrange("(t p) n -> p t n", p=P)).then_inc(mod_loaded, 16)

        @block.vector
        def _(dve):
            for b in range(NB):
                tiles = range(b * TPB, (b + 1) * TPB)
                if x_sb is None:
                    dve.wait_ge(x_loaded[b], 16)
                for i in tiles:
                    dve.bn_stats(stats[:, i, :], x[:, i, :]).then_inc(stats_done, 1)
                for i in tiles:
                    dve.wait_ge(stats_done, i + 1)
                    dve.bn_aggr(mv[:, i, :], stats[:, i, :]).then_inc(aggr_done, 1)
                half = slice(b * TPB, (b + 1) * TPB)
                dve.wait_ge(aggr_done, (b + 1) * TPB)
                dve.tensor_scalar(std[:, half], mv[:, half, 1], EPS, None, ALU.add).then_inc(var_done, 1)
                dve.wait_ge(std_done, b + 1)
                dve.reciprocal(rstd[:, half], std[:, half]).then_inc(rstd_done, 1)
                dve.wait_ge(rstd_done, b + 1)
                for i in tiles:
                    dve.tensor_scalar(xn[:, i, :], x[:, i, :], mv[:, i, 0:1], rstd[:, i:i + 1],
                                      ALU.subtract, ALU.mult).then_inc(xn_done, 1)
            dve.wait_ge(mod_ready, 1)
            dve.tensor_copy(mod[:, :], ps_mod[:, 0:2 * KT]).then_inc(mod_copied, 1)
            dve.tensor_scalar(scale1[:, :], ps_mod[:, KT:2 * KT], 1.0, None, ALU.add).then_inc(mod_copied, 1)
            for n in range(NB * KT):
                b, kt = n // KT, n % KT
                c = slice(b * QB, (b + 1) * QB)
                dve.wait_ge(hi_done, n + 1)
                dve.tensor_tensor(hT_lo[:, kt, c], z[:, n % 2, :], f32(hT_hi[:, kt, c]),
                                  ALU.subtract).then_inc(lo_done, 1)

        @block.scalar
        def _(act):
            for b in range(NB):
                half = slice(b * TPB, (b + 1) * TPB)
                act.wait_ge(var_done, b + 1)
                act.activation(std[:, half], std[:, half], ACT.Sqrt).then_inc(std_done, 1)
            act.wait_ge(mod_loaded, 32)
            act.activation(c_silu[:, :], c_col[:, :], ACT.Silu).then_inc(silu_done, 1)
            act.wait_ge(mod_copied, 2)
            for n in range(NB * KT):
                b, kt = n // KT, n % KT
                act.wait_ge(turned, n + 1)
                if n >= 2:
                    act.wait_ge(lo_done, n - 1)
                act.activation(z[:, n % 2, :], ps_t[:, n % 2, :], ACT.Identity, bias=mod[:, kt:kt + 1],
                               scale=scale1[:, kt:kt + 1]).then_inc(modulated, 1)
                act.wait_ge(modulated, n + 1)
                act.copy(hT_hi[:, kt, b * QB:(b + 1) * QB], z[:, n % 2, :]).then_inc(hi_done, 1)

        @block.tensor
        def _(pe):
            pe.wait_ge(silu_done, 1)
            for j in range(2 * KT):
                for kt in range(KT):
                    mm = pe.matmul(ps_mod[:, j:j + 1], wmod[:, kt, j * P:(j + 1) * P], c_silu[:, kt:kt + 1],
                                   start=(kt == 0), stop=(kt == KT - 1))
            mm.then_inc(mod_ready, 1)
            for n in range(NB * KT):
                b, kt = n // KT, n % KT
                if kt == 0:
                    pe.wait_ge(xn_done, (b + 1) * TPB)
                if n >= 2:
                    pe.wait_ge(modulated, n - 1)
                for t in range(TPB):
                    mm = pe.transpose(ps_t[:, n % 2, t * P:(t + 1) * P], xn[:, b * TPB + t, kt * P:(kt + 1) * P],
                                      ident[:, :])
                mm.then_inc(turned, 1)


def chunks_of(n):
    b, t = n // (HPG * TPB), n % TPB
    first = n if b == 0 else HPG * TPB + 2 * (n - HPG * TPB)
    width = b * TPB + t + 1
    return [(first + k, TPB * k, min(TPB, width - TPB * k)) for k in range(b + 1)]


CHUNKS = HPG * TPB * 3


def attention_phase(nc, hT_hi, hT_lo, acc, ident, identb, maskb, wjobs, sjobs, cos_dram, sin_dram, r_scratch):
    ctx = ExitStack()
    with ctx:
        al = Allocator(nc, ctx)
        sbuf, psum, sem = al.sbuf, al.psum, al.sem

        cosT, sinT = sbuf("cosT", [P, S]), sbuf("sinT", [P, S])
        kT_hi, kT_lo = sbuf("kT_hi", [P, S], F32R), sbuf("kT_lo", [P, S], F32R)
        v_hi, v_lo = sbuf("v_hi", [P, ST, HD], F32R), sbuf("v_lo", [P, ST, HD], F32R)
        wk_hi, wk_lo = sbuf("wk_hi", [P, KT, HD], F32R), sbuf("wk_lo", [P, KT, HD], F32R)
        wv_hi, wv_lo = sbuf("wv_hi", [P, KT, HD], F32R), sbuf("wv_lo", [P, KT, HD], F32R)
        wq_hi = [sbuf(f"wq_hi{h}", [P, KT, HD], F32R) for h in range(HPG)]
        wq_lo = [sbuf(f"wq_lo{h}", [P, KT, HD], F32R) for h in range(HPG)]
        wo_hi = [sbuf(f"wo_hi{h}", [P, H], F32R) for h in range(HPG)]
        wo_lo = [sbuf(f"wo_lo{h}", [P, H], F32R) for h in range(HPG)]
        w_int, w_scale = sbuf("w_int", [P, 2, H], I32), sbuf("w_scale", [P, 2, H])
        w_full = sbuf("w_full", [P, 2, H])
        qT_hi, qT_lo = sbuf("qT_hi", [P, 2, QB], F32R), sbuf("qT_lo", [P, 2, QB], F32R)
        swapped, roped = sbuf("swapped", [P, QB]), sbuf("roped", [P, QB])
        cosed, sined = sbuf("cosed", [P, QB]), sbuf("sined", [P, QB])
        probs = sbuf("probs", [P, 2, S])
        vT = probs[:, 0, :]
        roped_k = sbuf("roped_k", [P, NB, QB])
        pT_hi, pT_lo = sbuf("pT_hi", [P, ST, QB], F32R), sbuf("pT_lo", [P, ST, QB], F32R)
        ctx_hi, ctx_lo = sbuf("ctx_hi", [P, HPG, QB], F32R), sbuf("ctx_lo", [P, HPG, QB], F32R)
        ctx_full = sbuf("ctx_full", [P, QB])
        r_spread = sbuf("r_spread", [P, 2, QB])
        neg_max = sbuf("neg_max", [P, 2])
        row_sum = sbuf("row_sum", [P, 2, TPB])
        row_recip = sbuf("row_recip", [P, 2, TPB])

        ps = psum("ps", [P, 8, 512])
        SCORES = [ps[:, 0:2, :].rearrange("p a n -> p (a n)"), ps[:, 2:4, :].rearrange("p a n -> p (a n)")]
        TURN, CTX, PROJ = [ps[:, 4, :], ps[:, 5, :]], ps[:, 6, :], ps[:, 7, :]

        tables_loaded = sem("tables_loaded")
        w_loaded = [sem("w_loaded0"), sem("w_loaded1")]
        w_dequant, w_hi_done, w_lo_done = sem("w_dequant"), sem("w_hi_done"), sem("w_lo_done")
        k_proj, k_swapped, k_cos, k_sin, k_roped, k_hi_done, k_lo_done = (
            sem(n) for n in ("k_proj", "k_swapped", "k_cos", "k_sin", "k_roped", "k_hi_done", "k_lo_done"))
        v_proj, v_copied, v_turned, v_hi_done, v_lo_done = (
            sem(n) for n in ("v_proj", "v_copied", "v_turned", "v_hi_done", "v_lo_done"))
        q_proj, q_swapped, q_cos, q_sin, q_roped, q_hi_done, q_lo_done = (
            sem(n) for n in ("q_proj", "q_swapped", "q_cos", "q_sin", "q_roped", "q_hi_done", "q_lo_done"))
        scores_ready, max_ready, probs_ready = sem("scores_ready"), sem("max_ready"), sem("probs_ready")
        turn_ready, turn_hi, turn_lo = sem("turn_ready"), sem("turn_hi"), sem("turn_lo")
        recip_ready, r_stored, r_loaded = sem("recip_ready"), sem("r_stored"), sem("r_loaded")
        ctx_ready, ctx_scaled, ctx_hi_done, ctx_lo_done = (
            sem(n) for n in ("ctx_ready", "ctx_scaled", "ctx_hi_done", "ctx_lo_done"))
        out_ready, out_added = sem("out_ready"), sem("out_added")

        block = ctx.enter_context(nc.Block())

        PV_AT = (0, 2)
        OUT_AT = HPG + 1
        OUT_SLOTS = ((0, 1), (0, 2), (1, 0), (1, 1))

        def over_groups(eng, body):
            body(0, True, False)
            with eng.Fori(1, NKV - 1) as g:
                body(g, False, False)
            body(NKV - 1, False, True)

        JOBS_IN = ([], [], [JWO], [JWO + 1, JWO + 2], [JWO + 3, JWQ], [JWK, JWQ + 1], [JWV, JWQ + 2], [JWQ + 3])
        AHEAD = JWO

        def jobs_in(g, u, last):
            before = sum(len(x) for x in JOBS_IN[:u])
            jobs = []
            for i, k in enumerate(JOBS_IN[u]):
                if k >= JWO:
                    jobs.append((g, k, AHEAD + g * JOBS + before + i, (before + i) % 2))
                elif not last:
                    jobs.append((g + 1, k, AHEAD + g * JOBS + before + i, (before + i) % 2))
            return jobs

        def all_jobs(g, last):
            return [j for u in range(UNITS) for j in jobs_in(g, u, last)]

        def out_tile(g, u, t, first):
            if u == 0:
                return None if first else (1, t, g * ST - TPB + t, CTX)
            if (u - OUT_AT, t) in OUT_SLOTS:
                i = OUT_SLOTS.index((u - OUT_AT, t))
                return 0, i, g * ST + i, PROJ
            return None

        def q_quarters(u, t, last):
            if last and u + 2 >= UNITS:
                return []
            if u == OUT_AT:
                return {3: [0, 1, 2, 3]}.get(t, [])
            if u == OUT_AT + 1:
                return {2: [0, 1], 3: [2, 3]}.get(t, [])
            return {1: [0, 1], 2: [2], 3: [3]}.get(t, [])

        def ctx_split_slot(u):
            return (u + 2, 2) if u == HPG else (u + 2, 0)

        def w_parts(k):
            if k == JWK:
                hi, lo = wk_hi, wk_lo
            elif k == JWV:
                hi, lo = wv_hi, wv_lo
            elif k < JWO:
                hi, lo = wq_hi[k - JWQ], wq_lo[k - JWQ]
            else:
                return wo_hi[k - JWO][:, :], wo_lo[k - JWO][:, :]
            return hi[:, :, :].rearrange("p t n -> p (t n)"), lo[:, :, :].rearrange("p t n -> p (t n)")

        def turned_parts(n, j0, nj):
            b, t = n // (HPG * TPB), n % TPB
            at = j0 + TPB * (1 - b)
            return pT_hi[:, at:at + nj, t * P:(t + 1) * P], pT_lo[:, at:at + nj, t * P:(t + 1) * P]

        def chunk(bank, nj):
            return TURN[bank][:, 0:nj * P].rearrange("p (j q) -> p j q", q=P)

        KEYS, VALUES = [ps[:, 0, :], ps[:, 1, :]], [ps[:, 2, :], ps[:, 3, :]]
        VTURN = ps[:, 4:6, :].rearrange("p a n -> p (a n)")

        @block.sync
        def _(sp):
            def load_job(g, k, slot):
                sp.dma_start(w_int[:, slot, :], wjobs[g, k]).then_inc(w_loaded[slot], 16)
                sp.dma_start(w_scale[:, slot, :], sjobs[g, k].partition_broadcast(P)).then_inc(w_loaded[slot], 16)

            def spread_recip(g, u, loads):
                sp.wait_ge(recip_ready, g * UNITS + u + 1)
                sp.dma_start(r_scratch[u % 2].rearrange("(t p) -> p t", p=P), row_recip[:, u % 2, :],
                             allow_slow_non_contiguous=True).then_inc(r_stored, 16)
                for job in loads:
                    load_job(*job)
                sp.wait_ge(r_stored, (g * UNITS + u + 1) * 16)
                sp.dma_start(r_spread[:, u % 2, :], r_scratch[u % 2].partition_broadcast(P)).then_inc(r_loaded, 16)

            for k in range(AHEAD):
                if k >= 2:
                    sp.wait_ge(w_dequant, k - 1)
                load_job(0, k, k % 2)
                if k == 1:
                    sp.dma_start(cosT[:, :], cos_dram).then_inc(tables_loaded, 16)
                    sp.dma_start(sinT[:, :], sin_dram).then_inc(tables_loaded, 16)
            for g, k, number, slot in all_jobs(0, False)[:2]:
                sp.wait_ge(w_dequant, number - 1)
                load_job(g, k, slot)

            def body(g, first, last):
                jobs = [(x[0], x[1]) for x in all_jobs(g, last)[2:]]
                if not last:
                    jobs += [(g + 1, JWO), (g + 1, JWO + 1)]
                for u in range(UNITS):
                    done = jobs_in(g, u, last)
                    loads = [(*jobs.pop(0), x[3]) for x in done if jobs]
                    spread_recip(g, u, loads)
            over_groups(sp, body)

        @block.gpsimd
        def _(pool):
            pool.memset(f32(pT_hi[:, 5, 0:P]), 0.0)
            pool.memset(f32(pT_lo[:, 5, 0:P]), 0.0)
            pool.memset(f32(pT_hi[:, 7, 2 * P:3 * P]), 0.0)
            pool.memset(f32(pT_lo[:, 7, 2 * P:3 * P]), 0.0).then_inc(ctx_lo_done, 1)

            def w_lo(number, k, slot):
                hi, lo = w_parts(k)
                pool.wait_ge(w_hi_done, number + 1)
                pool.tensor_tensor(lo, w_full[:, slot, :], f32(hi), ALU.subtract).then_inc(w_lo_done, 1)

            def q_add(unit):
                pool.wait_ge(q_sin, unit + 1)
                pool.tensor_tensor(roped[:, :], cosed[:, :], sined[:, :], ALU.add).then_inc(q_roped, 1)

            def ctx_lo_part(g, u):
                pool.wait_ge(ctx_hi_done, g * UNITS + u + 1)
                pool.tensor_tensor(ctx_lo[:, u % HPG, :], ctx_full[:, :], f32(ctx_hi[:, u % HPG, :]),
                                   ALU.subtract).then_inc(ctx_lo_done, 1)

            for k in range(AHEAD):
                w_lo(k, k, k % 2)
            q_add(0)

            def body(g, first, last):
                for u in range(UNITS):
                    if not (last and u == UNITS - 1):
                        if not (isinstance(g, int) and g == 0 and u == 0):
                            pool.wait_ge(q_lo_done, g * UNITS + u + 1)
                        else:
                            pool.wait_ge(q_lo_done, 1)
                        q_add(g * UNITS + u + 1)
                    for w in range(UNITS):
                        if ctx_split_slot(w)[0] == u:
                            ctx_lo_part(g, w)
                    for _, k, number, slot in jobs_in(g, u, last):
                        w_lo(number, k, slot)
                ctx_lo_part(g, UNITS - 2)
                ctx_lo_part(g, UNITS - 1)
            over_groups(pool, body)

        @block.scalar
        def _(act):
            def w_hi(number, k, slot):
                act.wait_ge(w_dequant, number + 1)
                act.copy(w_parts(k)[0], w_full[:, slot, :]).then_inc(w_hi_done, 1)

            def swap_halves(src):
                act.copy(swapped[0:64, :], src[64:128, :])
                return act.copy(swapped[64:128, :], src[0:64, :])

            def q_swap(unit, src):
                act.wait_ge(q_proj, unit + 1)
                swap_halves(src).then_inc(q_swapped, 1)

            def q_hi(unit, u):
                act.wait_ge(q_roped, unit + 1)
                act.copy(qT_hi[:, u % 2, :], roped[:, :]).then_inc(q_hi_done, 1)

            def turn(g, n):
                for c, j0, nj in chunks_of(n):
                    act.wait_ge(turn_ready, g * CHUNKS + c + 1)
                    act.copy(turned_parts(n, j0, nj)[0], chunk(c % 2, nj)).then_inc(turn_hi, 1)

            def ctx_hi_part(g, u):
                act.wait_ge(ctx_scaled, g * UNITS + u + 1)
                if u == HPG:
                    act.wait_ge(out_ready, g * ST + TPB)
                act.copy(ctx_hi[:, u % HPG, :], ctx_full[:, :]).then_inc(ctx_hi_done, 1)

            def k_swap(g, half):
                act.wait_ge(k_proj, g * NB + half + 1)
                if half:
                    act.wait_ge(k_sin, g * NB + half)
                swap_halves(KEYS[half]).then_inc(k_swapped, 1)

            def k_hi(g, half):
                act.wait_ge(k_roped, g * NB + half + 1)
                act.copy(kT_hi[:, half * QB:(half + 1) * QB], roped_k[:, half, :]).then_inc(k_hi_done, 1)

            def v_copy(g, half):
                act.wait_ge(v_proj, g * NB + half + 1)
                act.copy(vT[:, half * QB:(half + 1) * QB], VALUES[half]).then_inc(v_copied, 1)

            def v_hi_part(g):
                act.wait_ge(v_turned, g + 1)
                act.copy(v_hi[:, :, :].rearrange("p t d -> p (t d)"), VTURN).then_inc(v_hi_done, 1)

            for k in range(AHEAD):
                w_hi(k, k, k % 2)
            k_swap(0, 0)
            k_hi(0, 0)
            k_swap(0, 1)
            k_hi(0, 1)
            v_copy(0, 0)
            v_copy(0, 1)
            q_swap(0, CTX)
            v_hi_part(0)
            q_hi(0, 0)

            def body(g, first, last):
                for n in range(TILES):
                    u, t = n // TPB, n % TPB
                    width = (u // HPG * TPB + t + 1) * P
                    more = not (last and u == UNITS - 1)
                    if t == 0 and more:
                        q_swap(g * UNITS + u + 1, PROJ)
                    for w in range(UNITS):
                        if ctx_split_slot(w) == (u, t):
                            ctx_hi_part(g, w)
                    if t == 1 and more:
                        q_hi(g * UNITS + u + 1, u + 1)
                    jobs = jobs_in(g, u, last)
                    if 2 <= t < 2 + len(jobs):
                        _, k, number, slot = jobs[t - 2]
                        w_hi(number, k, slot)
                    if n >= 2:
                        turn(g, n - 2)
                    act.wait_ge(max_ready, g * TILES + n + 1)
                    act.activation(probs[:, n % 2, 0:width], SCORES[n % 2][:, 0:width], ACT.Exp,
                                   bias=neg_max[:, n % 2:n % 2 + 1], scale=-1.0,
                                   accum_out=row_sum[:, u % 2, t:t + 1]).then_inc(probs_ready, 1)
                ctx_hi_part(g, UNITS - 2)
                if not last:
                    k_swap(g + 1, 0)
                    k_swap(g + 1, 1)
                turn(g, TILES - 2)
                if not last:
                    k_hi(g + 1, 0)
                turn(g, TILES - 1)
                if not last:
                    k_hi(g + 1, 1)
                    v_copy(g + 1, 0)
                ctx_hi_part(g, UNITS - 1)
                if not last:
                    v_copy(g + 1, 1)
                    v_hi_part(g + 1)
            over_groups(act, body)

        @block.vector
        def _(dve):
            def dequant(g, k, number, slot, count):
                dve.wait_ge(w_loaded[slot], count * 32)
                if not (isinstance(number, int) and number < 2):
                    dve.wait_ge(w_lo_done, number - 1)
                dve.scalar_tensor_tensor(out=w_full[:, slot, :], in0=w_int[:, slot, :], scalar=-ZERO,
                                         in1=w_scale[:, slot, :], op0=ALU.add, op1=ALU.mult).then_inc(w_dequant, 1)

            def q_rope(unit, u, src, first=False):
                c = slice(u // HPG * QB, (u // HPG + 1) * QB)
                dve.wait_ge(q_swapped, unit + 1)
                if not first:
                    dve.wait_ge(q_roped, unit)
                dve.scalar_tensor_tensor(out=cosed[:, :], in0=src, scalar=-SCALE, in1=cosT[:, c],
                                         op0=ALU.mult, op1=ALU.mult).then_inc(q_cos, 1)
                dve.scalar_tensor_tensor(out=sined[:, :], in0=swapped[:, :], scalar=-SCALE, in1=sinT[:, c],
                                         op0=ALU.mult, op1=ALU.mult).then_inc(q_sin, 1)

            def q_lo_part(unit, u):
                dve.wait_ge(q_hi_done, unit + 1)
                dve.tensor_tensor(qT_lo[:, u % 2, :], roped[:, :], f32(qT_hi[:, u % 2, :]),
                                  ALU.subtract).then_inc(q_lo_done, 1)

            def k_rope(g, half):
                c = slice(half * QB, (half + 1) * QB)
                i = g * NB + half + 1
                dve.wait_ge(k_swapped, i)
                dve.tensor_tensor(roped_k[:, half, :], KEYS[half], cosT[:, c], ALU.mult).then_inc(k_cos, 1)
                if not isinstance(g, int) or g:
                    dve.wait_ge(q_roped, g * UNITS + 1)
                dve.tensor_tensor(sined[:, :], swapped[:, :], sinT[:, c], ALU.mult).then_inc(k_sin, 1)
                dve.wait_ge(k_cos, i)
                dve.wait_ge(k_sin, i)
                dve.tensor_tensor(roped_k[:, half, :], roped_k[:, half, :], sined[:, :], ALU.add).then_inc(k_roped, 1)
                dve.wait_ge(k_roped, i)

            def k_lo_part(g, half):
                c = slice(half * QB, (half + 1) * QB)
                dve.wait_ge(k_hi_done, g * NB + half + 1)
                dve.tensor_tensor(kT_lo[:, c], roped_k[:, half, :], f32(kT_hi[:, c]), ALU.subtract).then_inc(k_lo_done, 1)

            def v_lo_part(g):
                dve.wait_ge(v_hi_done, g + 1)
                dve.tensor_tensor(v_lo[:, :, :].rearrange("p t d -> p (t d)"), VTURN,
                                  f32(v_hi[:, :, :].rearrange("p t d -> p (t d)")), ALU.subtract).then_inc(v_lo_done, 1)

            def turn(g, n):
                for c, j0, nj in chunks_of(n):
                    hi, lo = turned_parts(n, j0, nj)
                    dve.wait_ge(turn_hi, g * CHUNKS + c + 1)
                    dve.tensor_tensor(lo, chunk(c % 2, nj), f32(hi), ALU.subtract).then_inc(turn_lo, 1)

            def recip(g, u):
                dve.wait_ge(probs_ready, g * TILES + (u + 1) * TPB)
                dve.reciprocal(row_recip[:, u % 2, :], row_sum[:, u % 2, :]).then_inc(recip_ready, 1)

            def ctx_scale(g, u):
                dve.wait_ge(ctx_ready, g * UNITS + u + 1)
                dve.wait_ge(r_loaded, (g * UNITS + u + 1) * 16)
                dve.wait_ge(ctx_lo_done, g * UNITS + u + 1)
                dve.tensor_tensor(ctx_full[:, :], CTX, r_spread[:, u % 2, :], ALU.mult).then_inc(ctx_scaled, 1)

            def out_add(number, tile, src):
                dve.wait_ge(out_ready, number + 1)
                dve.tensor_tensor(acc[:, tile, :], src, acc[:, tile, :], ALU.add).then_inc(out_added, 1)

            dve.memset(acc[:, :, :], 0.0).then_inc(out_added, 1)
            dve.wait_ge(out_added, 1)
            for k in range(AHEAD):
                dequant(0, k, k, k % 2, k // 2 + 1)
            dve.wait_ge(tables_loaded, 32)
            for half in range(NB):
                k_rope(0, half)
                k_lo_part(0, half)
            q_rope(0, 0, CTX, first=True)
            v_lo_part(0)
            q_lo_part(0, 0)

            def body(g, first, last):
                pending = None
                for n in range(TILES):
                    u, t = n // TPB, n % TPB
                    width = (u // HPG * TPB + t + 1) * P
                    more = not (last and u == UNITS - 1)
                    if t == 0 and u:
                        recip(g, u - 1)
                    dve.wait_ge(scores_ready, g * TILES + n + 1)
                    dve.tensor_reduce(neg_max[:, n % 2:n % 2 + 1], SCORES[n % 2][:, 0:width], AX.X,
                                      ALU.min).then_inc(max_ready, 1)
                    if pending is not None:
                        b, i, number, bank = pending
                        out_add(number, b * TPB + i, bank)
                    pending = out_tile(g, u, t, first)
                    if t == 0 and more:
                        q_rope(g * UNITS + u + 1, (u + 1) % UNITS, PROJ)
                    if t == 2 and more:
                        q_lo_part(g * UNITS + u + 1, u + 1)
                    jobs = jobs_in(g, u, last)
                    if 1 <= t < 1 + len(jobs):
                        gj, k, number, slot = jobs[t - 1]
                        before = sum(len(x) for x in JOBS_IN[:u]) + t - 1
                        dequant(gj, k, number, slot, AHEAD // 2 + g * (JOBS // 2) + before // 2 + 1)
                    if t == 3 and u:
                        ctx_scale(g, u - 1)
                    if n >= 2:
                        turn(g, n - 2)
                recip(g, UNITS - 1)
                if not last:
                    k_rope(g + 1, 0)
                turn(g, TILES - 2)
                if not last:
                    k_rope(g + 1, 1)
                    k_lo_part(g + 1, 0)
                turn(g, TILES - 1)
                if not last:
                    k_lo_part(g + 1, 1)
                ctx_scale(g, UNITS - 1)
                if not last:
                    v_lo_part(g + 1)
                else:
                    for i in range(TPB):
                        out_add(NKV * ST - TPB + i, TPB + i, ps[:, i, :])
            over_groups(dve, body)

        @block.tensor
        def _(pe):
            def projected(out, w_hi, w_lo, b, tiles=range(KT)):
                c = slice(b * QB, (b + 1) * QB)
                for kt in tiles:
                    pe.matmul(out, w_hi[:, kt, :], hT_hi[:, kt, c], start=(kt == 0), stop=False)
                    pe.matmul(out, w_hi[:, kt, :], hT_lo[:, kt, c], start=False, stop=False)
                    mm = pe.matmul(out, w_lo[:, kt, :], hT_hi[:, kt, c], start=False, stop=(kt == KT - 1))
                return mm

            def scores(g, n):
                u, t = n // TPB, n % TPB
                i = (u // HPG) * TPB + t
                out = SCORES[n % 2]
                if t == 0:
                    pe.wait_ge(q_lo_done, g * UNITS + u + 1)
                if n == 0:
                    pe.wait_ge(k_lo_done, (g + 1) * NB)
                elif n >= 2:
                    pe.wait_ge(probs_ready, g * TILES + n - 1)
                width = (i + 1) * P
                q = slice(t * P, (t + 1) * P)
                for c0 in range(0, width, 512):
                    c = slice(c0, c0 + max(NSMALL, min(512, width - c0)))
                    pe.matmul(out[:, c], qT_hi[:, u % 2, q], kT_hi[:, c], start=True, stop=False)
                    pe.matmul(out[:, c], qT_hi[:, u % 2, q], kT_lo[:, c], start=False, stop=False)
                    pe.matmul(out[:, c], qT_lo[:, u % 2, q], kT_hi[:, c], start=False, stop=(c0 + 512 < width))
                pe.matmul(out[:, i * P:(i + 1) * P], identb, maskb, start=False, stop=True).then_inc(scores_ready, 1)

            def turn(g, n):
                pe.wait_ge(probs_ready, g * TILES + n + 1)
                for c, j0, nj in chunks_of(n):
                    if c >= 2:
                        pe.wait_ge(turn_lo, g * CHUNKS + c - 1)
                    else:
                        pe.wait_ge(v_lo_done, g + 1)
                    for j in range(nj):
                        mm = pe.transpose(TURN[c % 2][:, j * P:(j + 1) * P],
                                          probs[:, n % 2, (j0 + j) * P:(j0 + j + 1) * P], ident[:, :])
                    mm.then_inc(turn_ready, 1)

            def times_v(g, u, side):
                b = u // HPG
                last_chunk = chunks_of(u * TPB + 2 * side + 1)[-1][0]
                pe.wait_ge(turn_lo, g * CHUNKS + last_chunk + 1)
                if u == 0 and side == 0:
                    pe.wait_ge(out_added, 1 + g * ST)
                elif side == 0:
                    pe.wait_ge(ctx_scaled, g * UNITS + u)
                c = slice(side * 2 * P, (side + 1) * 2 * P)
                tiles = b * TPB + 2 * side + 2
                for j in range(tiles):
                    at = j + TPB * (1 - b)
                    pe.matmul(CTX[:, c], v_hi[:, j, :], pT_hi[:, at, c], start=(j == 0), stop=False)
                    pe.matmul(CTX[:, c], v_hi[:, j, :], pT_lo[:, at, c], start=False, stop=False)
                    mm = pe.matmul(CTX[:, c], v_lo[:, j, :], pT_hi[:, at, c], start=False, stop=(j == tiles - 1))
                if side == 1:
                    mm.then_inc(ctx_ready, 1)

            def project_out(tt, out):
                q = slice(tt * P, (tt + 1) * P)
                for h in range(HPG):
                    pe.matmul(out, ctx_hi[:, h, q], wo_hi[h][:, :], start=(h == 0), stop=False)
                    pe.matmul(out, ctx_hi[:, h, q], wo_lo[h][:, :], start=False, stop=False)
                    mm = pe.matmul(out, ctx_lo[:, h, q], wo_hi[h][:, :], start=False, stop=(h == HPG - 1))
                mm.then_inc(out_ready, 1)

            def keys(g):
                for half in range(NB):
                    projected(KEYS[half], wk_hi, wk_lo, half).then_inc(k_proj, 1)

            def values(g, half):
                projected(VALUES[half], wv_hi, wv_lo, half).then_inc(v_proj, 1)

            def turn_values(g):
                pe.wait_ge(v_copied, (g + 1) * NB)
                for j in range(ST):
                    mm = pe.transpose(VTURN[:, j * P:(j + 1) * P], vT[:, j * P:(j + 1) * P], ident[:, :])
                mm.then_inc(v_turned, 1)

            pe.wait_ge(ctx_lo_done, 1)
            pe.wait_ge(w_lo_done, 1)
            keys(0)
            pe.wait_ge(w_lo_done, 2)
            values(0, 0)
            values(0, 1)
            pe.wait_ge(w_lo_done, 3)
            projected(CTX, wq_hi[0], wq_lo[0], 0).then_inc(q_proj, 1)
            pe.wait_ge(w_lo_done, 4)
            projected(PROJ, wq_hi[1], wq_lo[1], 0).then_inc(q_proj, 1)
            turn_values(0)
            pe.wait_ge(w_lo_done, AHEAD)
            scores(0, 0)

            def body(g, first, last):
                for n in range(TILES):
                    u, t = n // TPB, n % TPB
                    if n + 1 < TILES:
                        scores(g, n + 1)
                    elif not last:
                        pe.wait_ge(probs_ready, g * TILES + n)
                        keys(g + 1)
                    if u and t in PV_AT:
                        times_v(g, u - 1, PV_AT.index(t))
                    tile = out_tile(g, u, t, first)
                    if tile is not None:
                        b, i, number, bank = tile
                        if i == 0:
                            pe.wait_ge(ctx_lo_done, 1 + (g * UNITS + HPG if b == 0 else g * UNITS))
                        if b == 0 and i in (0, 2):
                            pe.wait_ge(q_cos, g * UNITS + u + 2)
                        elif i:
                            pe.wait_ge(out_added, 1 + number)
                        project_out(i, bank)
                    quarters = q_quarters(u, t, last)
                    if quarters:
                        w = (u + 2) % UNITS
                        if quarters[0] == 0:
                            if u in (OUT_AT, OUT_AT + 1):
                                pe.wait_ge(out_added, 1 + g * ST + 2 * (u - OUT_AT + 1))
                            else:
                                pe.wait_ge(q_cos, g * UNITS + u + 2)
                            if u + 2 >= UNITS:
                                k = JWQ + w % HPG
                                number = [x[2] for x in all_jobs(g, last) if x[1] == k][0]
                                pe.wait_ge(w_lo_done, number + 1)
                        mm = projected(PROJ, wq_hi[w % HPG], wq_lo[w % HPG], w // HPG, quarters)
                        if quarters[-1] == KT - 1:
                            mm.then_inc(q_proj, 1)
                    if n:
                        turn(g, n - 1)
                turn(g, TILES - 1)
                if not last:
                    values(g + 1, 0)
                times_v(g, UNITS - 1, 0)
                times_v(g, UNITS - 1, 1)
                if not last:
                    values(g + 1, 1)
                    pe.wait_ge(turn_lo, (g + 1) * CHUNKS)
                    turn_values(g + 1)
                    scores(g + 1, 0)
                else:
                    pe.wait_ge(ctx_lo_done, 1 + NKV * UNITS)
                    for i in range(TPB):
                        project_out(i, ps[:, i, :])
            over_groups(pe, body)


def residual_phase(nc, tag, acc, gate, x_dram):
    ctx = ExitStack()
    with ctx:
        al = Allocator(nc, ctx)
        xin = al.sbuf(tag + "xin", [P, ST, H])
        x_loaded, scaled, added = al.sem(tag + "x_loaded"), al.sem(tag + "scaled"), al.sem(tag + "added")
        block = ctx.enter_context(nc.Block())

        @block.sync
        def _(sp):
            sp.dma_start(xin[:, :, :], x_dram.rearrange("(t p) n -> p t n", p=P)).then_inc(x_loaded, 16)

        @block.vector
        def _(dve):
            for i in range(ST):
                dve.tensor_tensor(acc[:, i, :], acc[:, i, :], gate, ALU.mult).then_inc(scaled, 1)
                if i == 0:
                    dve.wait_ge(x_loaded, 16)
                dve.wait_ge(scaled, i + 1)
                dve.tensor_tensor(acc[:, i, :], acc[:, i, :], xin[:, i, :], ALU.add).then_inc(added, 1)
            dve.wait_ge(added, ST)


def gate_phase(nc, gates, wga_dram, wgb_dram, c_dram):
    ctx = ExitStack()
    with ctx:
        al = Allocator(nc, ctx)
        wgate = al.sbuf("g_w", [P, KT, 2 * H])
        c_col, c_silu = al.sbuf("g_c", [P, KT]), al.sbuf("g_silu", [P, KT])
        sign, mag = al.sbuf("g_sign", [P, 2, H]), al.sbuf("g_mag", [P, 2, H])
        ps_g = al.psum("g_ps", [P, 2, 512])
        loaded, silu_done, ready, step = (al.sem("g_" + n) for n in ("loaded", "silu_done", "ready", "step"))
        block = ctx.enter_context(nc.Block())

        @block.sync
        def _(sp):
            sp.dma_start(c_col[:, :], c_dram).then_inc(loaded, 16)
            for i, w in enumerate((wga_dram, wgb_dram)):
                sp.dma_start(wgate[:, :, i * H:(i + 1) * H], w.rearrange("(t p) n -> p t n", p=P)).then_inc(loaded, 16)

        @block.scalar
        def _(act):
            act.wait_ge(loaded, 48)
            act.activation(c_silu[:, :], c_col[:, :], ACT.Silu).then_inc(silu_done, 1)

        @block.tensor
        def _(pe):
            pe.wait_ge(silu_done, 1)
            for i in range(2):
                for kt in range(KT):
                    mm = pe.matmul(ps_g[:, i, :], c_silu[:, kt:kt + 1].to_broadcast([P, P]),
                                   wgate[:, kt, i * H:(i + 1) * H], start=(kt == 0), stop=(kt == KT - 1))
            mm.then_inc(ready, 1)

        @block.vector
        def _(dve):
            dve.wait_ge(ready, 1)
            dve.tensor_scalar(sign[:, :, :], ps_g[:, :, :], 0.0, 2.0, ALU.is_ge, ALU.mult).then_inc(step, 1)
            dve.tensor_scalar(mag[:, :, :], ps_g[:, :, :], -1.0, None, ALU.mult).then_inc(step, 1)
            dve.wait_ge(step, 2)
            dve.tensor_tensor(mag[:, :, :], mag[:, :, :], ps_g[:, :, :], ALU.max).then_inc(step, 1)
            dve.wait_ge(step, 3)
            dve.tensor_scalar(mag[:, :, :], mag[:, :, :], 0.25, None, ALU.max).then_inc(step, 1)
            dve.wait_ge(step, 4)
            dve.scalar_tensor_tensor(out=gates[:, :, :], in0=sign[:, :, :], scalar=-1.0, in1=mag[:, :, :],
                                     op0=ALU.add, op1=ALU.mult).then_inc(step, 1)
            dve.wait_ge(step, 5)


def ffn_phase(nc, hT_hi, hT_lo, x, gate, ffn_dram, out_dram):
    ctx = ExitStack()
    with ctx:
        al = Allocator(nc, ctx)
        sbuf, psum, sem = al.sbuf, al.psum, (lambda n: al.sem("ffn_" + n))
        raw = sbuf("ffn_raw", [P, 2, 3 * H], F16)
        w_gu = [sbuf(f"ffn_w_gu{s}", [P, 2 * KT, P], F32R) for s in range(2)]
        w_down = [sbuf(f"ffn_w_down{s}", [P, H], F32R) for s in range(2)]
        gated, mid = sbuf("ffn_gated", [P, 2, QB]), sbuf("ffn_mid", [P, 2, QB])
        mid_hi = [sbuf(f"ffn_mid_hi{s}", [P, QB], F32R) for s in range(2)]
        mid_lo = [sbuf(f"ffn_mid_lo{s}", [P, QB], F32R) for s in range(2)]
        fin = sbuf("ffn_fin", [P, TPB, H])
        ps = psum("ffn_ps", [P, 8, 512])
        loaded = [sem("loaded0"), sem("loaded1")]
        gu_cast, down_cast, gate_up, silued, product, hi_done, lo_done, down = (
            sem(n) for n in ("gu_cast", "down_cast", "gate_up", "silued", "product", "hi_done", "lo_done", "down"))
        scaled, added, stored = sem("scaled"), sem("added"), sem("stored")
        block = ctx.enter_context(nc.Block())
        PAIRS = MT // 2

        def over_steps(eng, body, first=0, after=None):
            for b in range(NB):
                for i in range(first):
                    for s in range(2):
                        body(b, i, s)
                with eng.Fori(first, PAIRS - 1) as i:
                    for s in range(2):
                        body(b, i, s)
                for s in range(2):
                    body(b, PAIRS - 1, s)
                if after is not None:
                    after(b)

        @block.sync
        def _(sp):
            for s in range(2):
                sp.dma_start(raw[:, s, :], ffn_dram[s]).then_inc(loaded[s], 16)

            def body(b, i, s):
                if isinstance(i, int):
                    if b == NB - 1:
                        return
                    i_next = 0
                else:
                    i_next = i + 1
                sp.wait_ge(down_cast, b * MT + i * 2 + s + 1)
                sp.dma_start(raw[:, s, :], ffn_dram[i_next * 2 + s]).then_inc(loaded[s], 16)
            over_steps(sp, body)
            for b in range(NB):
                sp.wait_ge(added, (b + 1) * TPB)
                sp.dma_start(out_dram[b * QB:(b + 1) * QB, :].rearrange("(t p) n -> p t n", p=P),
                             x[:, b * TPB:(b + 1) * TPB, :]).then_inc(stored, 16)
            sp.wait_ge(stored, 16 * NB)

        @block.scalar
        def _(act):
            def body(b, i, s):
                m = b * MT + i * 2 + s
                act.wait_ge(gate_up, m + 1)
                act.activation(gated[:, s, :], ps[:, 2 * s, :], ACT.Silu).then_inc(silued, 1)
                act.wait_ge(product, m + 1)
                act.copy(mid_hi[s][:, :], mid[:, s, :]).then_inc(hi_done, 1)
            over_steps(act, body)

        @block.vector
        def _(dve):
            def cast_gu(count, s):
                dve.wait_ge(loaded[s], count * 16)
                dve.tensor_copy(w_gu[s][:, :, :].rearrange("p a n -> p (a n)"), raw[:, s, 0:2 * H]).then_inc(gu_cast, 1)

            def cast_down(s):
                dve.tensor_copy(w_down[s][:, :], raw[:, s, 2 * H:3 * H]).then_inc(down_cast, 1)

            def body(b, i, s):
                m = b * MT + i * 2 + s
                end = isinstance(i, int) and i == PAIRS - 1 and b == NB - 1
                dve.wait_ge(silued, m + 1)
                dve.tensor_tensor(mid[:, s, :], gated[:, s, :], ps[:, 2 * s + 1, :], ALU.mult).then_inc(product, 1)
                if not end:
                    cast_gu(b * PAIRS + i + 2, s)
                if not (end and s == 1):
                    if not (isinstance(m, int) and m == 0):
                        dve.wait_ge(down, m)
                    cast_down(1 - s)
                dve.wait_ge(hi_done, m + 1)
                dve.tensor_tensor(mid_lo[s][:, :], mid[:, s, :], f32(mid_hi[s][:, :]), ALU.subtract).then_inc(lo_done, 1)

            def after(b):
                dve.wait_ge(down, (b + 1) * MT)
                for t in range(TPB):
                    i = b * TPB + t
                    dve.tensor_tensor(fin[:, t, :], ps[:, 4 + t, :], gate, ALU.mult).then_inc(scaled, 1)
                    dve.wait_ge(scaled, i + 1)
                    dve.tensor_tensor(x[:, i, :], x[:, i, :], fin[:, t, :], ALU.add).then_inc(added, 1)

            cast_gu(1, 0)
            cast_gu(1, 1)
            cast_down(0)
            over_steps(dve, body, first=1, after=after)

        @block.tensor
        def _(pe):
            def project(b, i, s):
                m = b * MT + i * 2 + s
                pe.wait_ge(gu_cast, m + 1)
                if not (isinstance(i, int) and i == 0 and b == 0):
                    pe.wait_ge(product, m - 1)
                c = slice(b * QB, (b + 1) * QB)
                for a in range(2):
                    for kt in range(KT):
                        pe.matmul(ps[:, 2 * s + a, :], w_gu[s][:, a * KT + kt, :], hT_hi[:, kt, c],
                                  start=(kt == 0), stop=False)
                        mm = pe.matmul(ps[:, 2 * s + a, :], w_gu[s][:, a * KT + kt, :], hT_lo[:, kt, c],
                                       start=False, stop=(kt == KT - 1))
                mm.then_inc(gate_up, 1)

            def project_down(m, s, first=False, last=False):
                pe.wait_ge(lo_done, m + 1)
                for t in range(TPB):
                    q = slice(t * P, (t + 1) * P)
                    pe.matmul(ps[:, 4 + t, :], mid_hi[s][:, q], w_down[s][:, :], start=first, stop=False)
                    mm = pe.matmul(ps[:, 4 + t, :], mid_lo[s][:, q], w_down[s][:, :], start=False, stop=last)
                mm.then_inc(down, 1)

            def body(b, i, s):
                project(b, i, s)
                m = b * MT + i * 2 + s
                if isinstance(i, int) and i == 0 and s == 0:
                    return
                first = isinstance(i, int) and i == 0
                if first and b:
                    pe.wait_ge(added, b * TPB)
                project_down(m - 1, 1 - s, first=first)

            def after(b):
                project_down((b + 1) * MT - 1, 1, last=True)
            over_steps(pe, body, first=1, after=after)


def build(nc, x, wmod, c, wjobs, sjobs, ffn, cos, sin, ident_dram, masks_dram, r_scratch, out):
    ctx = ExitStack()
    with ctx:
        al = Allocator(nc, ctx)
        hT_hi, hT_lo = al.sbuf("hT_hi", [P, KT, S], F32R), al.sbuf("hT_lo", [P, KT, S], F32R)
        acc = al.sbuf("acc", [P, ST, H])
        ident = al.sbuf("ident", [P, P])
        masks = al.sbuf("masks", [P, 2, P], BF16)
        consts_loaded = al.sem("consts_loaded")
        with nc.Block() as block:
            @block.sync
            def _(sp):
                sp.dma_start(ident[:, :], ident_dram).then_inc(consts_loaded, 16)
                sp.dma_start(masks[:, :, :], masks_dram).then_inc(consts_loaded, 16)
                sp.wait_ge(consts_loaded, 32)
        normalise_phase(nc, "n1_", x, None, wmod[:, 0:2 * H], c, ident, hT_hi, hT_lo)
        attention_phase(nc, hT_hi, hT_lo, acc, ident, masks[:, 0, :], masks[:, 1, :], wjobs, sjobs, cos, sin, r_scratch)
        gates = al.sbuf("gates", [P, 2, H])
        gate_phase(nc, gates, wmod[:, 2 * H:3 * H], wmod[:, 5 * H:6 * H], c)
        residual_phase(nc, "r1_", acc, gates[:, 0, :], x)
        normalise_phase(nc, "n2_", None, acc, wmod[:, 3 * H:5 * H], c, ident, hT_hi, hT_lo)
        ffn_phase(nc, hT_hi, hT_lo, acc, gates[:, 1, :], ffn, out)


def kernel(L0_attn_hidden_states, L0_attn_scales_q, L0_attn_scales_k, L0_attn_scales_v, L0_attn_scales_o,
           L0_attn_qw_q, L0_attn_qw_k, L0_attn_qw_v, L0_attn_qw_o, L0_ffn_W_gate, L0_ffn_W_up, L0_ffn_W_down,
           L0_c, L0_wmod):
    import numpy as np
    import concourse.bacc as bacc
    from concourse.bass_utils import run_bass_kernel_spmd

    def by_head(w, heads):
        return w.reshape(-1, P, heads, HD).transpose(2, 1, 0, 3).reshape(heads, P, -1)

    def scale_by_head(s, heads):
        return s.reshape(KT, heads, HD).transpose(1, 0, 2).reshape(heads, H)

    def jobs(k, v, q, o):
        return np.ascontiguousarray(np.concatenate(
            [k[:, None], v[:, None], q.reshape(NKV, HPG, *q.shape[1:]), o.reshape(NKV, HPG, *o.shape[1:])], axis=1))

    def array(a):
        return np.asarray(a)

    wjobs = jobs(by_head(array(L0_attn_qw_k), NKV), by_head(array(L0_attn_qw_v), NKV),
                 by_head(array(L0_attn_qw_q), NH), array(L0_attn_qw_o).reshape(NH, HD, H))
    sjobs = jobs(scale_by_head(array(L0_attn_scales_k), NKV), scale_by_head(array(L0_attn_scales_v), NKV),
                 scale_by_head(array(L0_attn_scales_q), NH), array(L0_attn_scales_o))

    def ffn_side(w):
        return w.reshape(MT, P, KT, P).transpose(0, 3, 2, 1).reshape(MT, P, H)

    ffn = np.ascontiguousarray(np.concatenate(
        [ffn_side(array(L0_ffn_W_gate)), ffn_side(array(L0_ffn_W_up)),
         array(L0_ffn_W_down).T.reshape(MT, P, H)], axis=2))

    inv_freq = np.float32(1.0) / (10000.0 ** (np.arange(0, HD, 2) / HD)).astype(np.float32)
    angle = (np.arange(S, dtype=np.float32)[:, None] * inv_freq).astype(np.float64)
    cos = np.ascontiguousarray(np.concatenate([np.cos(angle), np.cos(angle)], axis=1).T.astype(np.float32))
    sin = np.ascontiguousarray(np.concatenate([-np.sin(angle), np.sin(angle)], axis=1).T.astype(np.float32))
    bf16 = mybir.dt.np(BF16)
    masks = np.zeros((P, 2, P), bf16)
    masks[:, 0] = np.eye(P)
    masks[:, 1] = np.triu(np.full((P, P), 1e37), 1)

    arrays = {"x": array(L0_attn_hidden_states)[0], "wmod": array(L0_wmod), "c": np.ascontiguousarray(array(L0_c).reshape(KT, P).T), "wjobs": wjobs,
              "sjobs": sjobs, "ffn": ffn, "cos": cos, "sin": sin, "ident": np.eye(P, dtype=np.float32), "masks": masks}
    nc = bacc.Bacc("TRN2", target_bir_lowering=False, num_devices=1)
    aps = {n: nc.dram_tensor("in_" + n, a.shape, mybir.dt.from_np(a.dtype), kind="ExternalInput").ap()
           for n, a in arrays.items()}
    r_scratch = nc.dram_tensor("r_scratch", (2, QB), F32, kind="Internal").ap()
    out = nc.dram_tensor("out", (S, H), F32, kind="ExternalOutput").ap()
    build(nc, aps["x"], aps["wmod"], aps["c"], aps["wjobs"], aps["sjobs"], aps["ffn"], aps["cos"], aps["sin"],
          aps["ident"], aps["masks"], r_scratch, out)
    r = run_bass_kernel_spmd(nc, [{"in_" + n: a for n, a in arrays.items()}], core_ids=[0])
    return r.results[0]["out"].reshape(1, S, H)
```

```python
from contextlib import ExitStack

import concourse.bass as bass
from concourse import mybir

ALU = mybir.AluOpType
ACT = mybir.ActivationFunctionType
AX = mybir.AxisListType
F32 = mybir.dt.float32
F32R = mybir.dt.float32r
BF16 = mybir.dt.bfloat16
F16 = mybir.dt.float16
I32 = mybir.dt.int32

P = 128
S, H = 1024, 512
NH, NKV, HD = 32, 8, 128
HPG = NH // NKV
M = 1792
KT = H // P
ST = S // P
QB = 512
NB = S // QB
TPB = QB // P
UNITS = NB * HPG
TILES = UNITS * TPB
JOBS = 2 + 2 * HPG
JWK, JWV, JWQ, JWO = 0, 1, 2, 2 + HPG
SCALE = float(HD) ** -0.5
EPS = 1e-5
ZERO = 8.0
MT = M // P
NSMALL = 256


def f32(ap):
    return ap.bitcast(F32)


class Allocator:
    def __init__(self, nc, ctx):
        self.nc, self.ctx = nc, ctx

    def sbuf(self, name, shape, dt=F32):
        return self.ctx.enter_context(self.nc.sbuf_tensor(name, shape, dt))

    def sbuf_shared(self, name, shape, shared_shape=None):
        with self.nc.sbuf_tensor(name + "_place", shared_shape or shape, F32) as place:
            pass
        return self.sbuf(name, shape, F32R), place

    def psum(self, name, shape, dt=F32):
        return self.ctx.enter_context(self.nc.psum_tensor(name, shape, dt))

    def sem(self, name):
        return self.ctx.enter_context(self.nc.semaphore(name))


class Normalise:
    def __init__(self, nc, al, tag, x, xn, z, banks, shift, scale1, ident, hT_hi, hT_lo):
        self.nc, self.x, self.xn, self.z, self.banks, self.shift, self.scale1 = nc, x, xn, z, banks, shift, scale1
        self.ident, self.hT_hi, self.hT_lo = ident, hT_hi, hT_lo
        self.stats, self.mv = al.sbuf(tag + "stats", [P, ST, 6]), al.sbuf(tag + "mv", [P, ST, 2])
        self.var, self.std = al.sbuf(tag + "var", [P, ST]), al.sbuf(tag + "std", [P, ST])
        self.rstd, self.fix = al.sbuf(tag + "rstd", [P, ST]), al.sbuf(tag + "fix", [P, ST])
        (self.stats_done, self.aggr_done, self.var_done, self.std_done, self.rstd_done, self.xn_done, self.turned,
         self.modulated, self.hi_done, self.lo_done) = (
            al.sem(tag + n) for n in ("stats_done", "aggr_done", "var_done", "std_done", "rstd_done", "xn_done",
                                      "turned", "modulated", "hi_done", "lo_done"))

    def tokens_dve(self, dve, b):
        x, mv, var, std, rstd, fix = self.x, self.mv, self.var, self.std, self.rstd, self.fix
        tiles, half = range(b * TPB, (b + 1) * TPB), slice(b * TPB, (b + 1) * TPB)
        for i in tiles:
            dve.bn_stats(self.stats[:, i, :], x[:, i, :]).then_inc(self.stats_done, 1)
        for i in tiles:
            dve.wait_ge(self.stats_done, i + 1)
            dve.bn_aggr(mv[:, i, :], self.stats[:, i, :]).then_inc(self.aggr_done, 1)
        dve.wait_ge(self.aggr_done, (b + 1) * TPB)
        dve.tensor_scalar(var[:, half], mv[:, half, 1], EPS, None, ALU.add).then_inc(self.var_done, 1)
        step = 5 * b
        dve.wait_ge(self.std_done, b + 1)
        dve.reciprocal(rstd[:, half], std[:, half]).then_inc(self.rstd_done, 1)
        dve.wait_ge(self.rstd_done, step + 1)
        dve.tensor_tensor(fix[:, half], rstd[:, half], rstd[:, half], ALU.mult).then_inc(self.rstd_done, 1)
        dve.wait_ge(self.rstd_done, step + 2)
        dve.tensor_tensor(fix[:, half], fix[:, half], var[:, half], ALU.mult).then_inc(self.rstd_done, 1)
        dve.wait_ge(self.rstd_done, step + 3)
        dve.tensor_scalar(fix[:, half], fix[:, half], -0.5, 1.5, ALU.mult, ALU.add).then_inc(self.rstd_done, 1)
        dve.wait_ge(self.rstd_done, step + 4)
        dve.tensor_tensor(rstd[:, half], rstd[:, half], fix[:, half], ALU.mult).then_inc(self.rstd_done, 1)
        dve.wait_ge(self.rstd_done, step + 5)
        for i in tiles:
            dve.tensor_scalar(self.xn[:, i, :], x[:, i, :], mv[:, i, 0:1], rstd[:, i:i + 1],
                              ALU.subtract, ALU.mult).then_inc(self.xn_done, 1)

    def root_act(self, act, b):
        half = slice(b * TPB, (b + 1) * TPB)
        act.wait_ge(self.var_done, b + 1)
        act.activation(self.std[:, half], self.var[:, half], ACT.Sqrt).then_inc(self.std_done, 1)

    def piece_pe(self, pe, n):
        b, kt = n // KT, n % KT
        if kt == 0:
            pe.wait_ge(self.xn_done, (b + 1) * TPB)
        if n >= 2:
            pe.wait_ge(self.modulated, n - 1)
        for t in range(TPB):
            mm = pe.transpose(self.banks[n % 2][:, t * P:(t + 1) * P],
                              self.xn[:, b * TPB + t, kt * P:(kt + 1) * P], self.ident[:, :])
        mm.then_inc(self.turned, 1)

    def piece_act(self, act, n):
        b, kt = n // KT, n % KT
        act.wait_ge(self.turned, n + 1)
        if n >= 2:
            act.wait_ge(self.lo_done, n - 1)
        act.activation(self.z[:, n % 2, :], self.banks[n % 2], ACT.Identity, bias=self.shift[:, kt:kt + 1],
                       scale=self.scale1[:, kt:kt + 1]).then_inc(self.modulated, 1)
        act.wait_ge(self.modulated, n + 1)
        act.copy(self.hT_hi[:, kt, b * QB:(b + 1) * QB], self.z[:, n % 2, :]).then_inc(self.hi_done, 1)

    def piece_lo(self, eng, n):
        b, kt = n // KT, n % KT
        c = slice(b * QB, (b + 1) * QB)
        eng.wait_ge(self.hi_done, n + 1)
        eng.tensor_tensor(self.hT_lo[:, kt, c], self.z[:, n % 2, :], f32(self.hT_hi[:, kt, c]),
                          ALU.subtract).then_inc(self.lo_done, 1)


def chunks_of(n):
    b, t = n // (HPG * TPB), n % TPB
    first = n if b == 0 else HPG * TPB + 2 * (n - HPG * TPB)
    width = b * TPB + t + 1
    return [(first + k, TPB * k, min(TPB, width - TPB * k)) for k in range(b + 1)]


CHUNKS = HPG * TPB * 3


def attention_phase(nc, hT_hi, hT_lo, acc, ident, masks, pT_hi, pT_lo, x, mod_cols, x_again, x_dram, wmod_dram, c_dram,
                    wjobs, sjobs, cos_dram, sin_dram, ident_dram, masks_dram, r_scratch):
    identb, maskb = masks[:, 0, :], masks[:, 1, :]
    ctx = ExitStack()
    with ctx:
        al = Allocator(nc, ctx)
        sbuf, psum, sem = al.sbuf, al.psum, al.sem

        cosT, sinT = sbuf("cosT", [P, S]), sbuf("sinT", [P, S])
        kT_hi, kT_lo = sbuf("kT_hi", [P, S], F32R), sbuf("kT_lo", [P, S], F32R)
        v_hi, v_lo = sbuf("v_hi", [P, ST, HD], F32R), sbuf("v_lo", [P, ST, HD], F32R)
        kv_parts = [al.sbuf_shared(n, [P, KT, HD], [P, H]) for n in ("wk_hi", "wk_lo", "wv_hi", "wv_lo")]
        q_parts = [[al.sbuf_shared(f"wq_{n}{h}", [P, KT, HD], [P, H]) for n in ("hi", "lo")] for h in range(HPG)]
        (wk_hi, wk_lo, wv_hi, wv_lo), kv_places = [x[0] for x in kv_parts], [x[1] for x in kv_parts]
        wq_hi, wq_lo = [x[0][0] for x in q_parts], [x[1][0] for x in q_parts]
        q_places = [[part[1] for x in q_parts[h:h + 2] for part in x] for h in (0, 2)]
        wo_hi = [sbuf(f"wo_hi{h}", [P, H], F32R) for h in range(HPG)]
        wo_lo = [sbuf(f"wo_lo{h}", [P, H], F32R) for h in range(HPG)]
        w_int, w_scale = sbuf("w_int", [P, 2, H], I32), sbuf("w_scale", [P, 2, H])
        w_full = sbuf("w_full", [P, 2, H])
        qT_hi, qT_lo = sbuf("qT_hi", [P, 2, QB], F32R), sbuf("qT_lo", [P, 2, QB], F32R)
        swapped, roped = sbuf("swapped", [P, QB]), sbuf("roped", [P, QB])
        cosed, sined = sbuf("cosed", [P, QB]), sbuf("sined", [P, QB])
        probs = sbuf("probs", [P, 2, S])
        vT = probs[:, 0, :]
        roped_k = sbuf("roped_k", [P, NB, QB])
        (ctx_hi, w_shift), (ctx_lo, w_scale1) = (al.sbuf_shared(n, [P, HPG, QB]) for n in ("ctx_hi", "ctx_lo"))
        ctx_full = sbuf("ctx_full", [P, QB])
        r_spread = sbuf("r_spread", [P, 2, QB])
        neg_max = sbuf("neg_max", [P, 2])
        mod_sign, mod_mag = sbuf("mod_sign", [P, 2 * KT]), sbuf("mod_mag", [P, 2 * KT])
        row_sum = sbuf("row_sum", [P, 2, TPB])
        row_recip = sbuf("row_recip", [P, 2, TPB])

        ps = psum("ps", [P, 8, 512])
        SCORES = [ps[:, 0:2, :].rearrange("p a n -> p (a n)"), ps[:, 2:4, :].rearrange("p a n -> p (a n)")]
        TURN, CTX, PROJ = [ps[:, 4, :], ps[:, 5, :]], ps[:, 6, :], ps[:, 7, :]

        xn = acc
        z = probs[:, 0, :].rearrange("p (a n) -> p a n", n=QB)
        mod1_rows = probs[:, 1, :].rearrange("p (a n) -> p a n", n=H)
        c_col, c_silu, ones = sbuf("c_col", [P, KT]), sbuf("c_silu", [P, KT]), sbuf("ones", [P, 1])
        mod1 = sbuf("mod1", [P, 2 * KT])
        norm = Normalise(nc, al, "n1_", x, xn, z, TURN, mod1[:, 0:KT], mod1[:, KT:2 * KT], ident, hT_hi, hT_lo)
        MOD2 = [(2, kv_places, roped_k[:, 0, :]),
                (5, kv_places, roped_k[:, 1, :]),
                (3, q_places[0], w_scale[:, 0, :]),
                (4, q_places[1], w_scale[:, 1, :])]
        MOD2_LOAD, MOD2_SUM = (0, 3, 4, 5), (2, 4, 6, 7)

        c_loaded, consts_loaded, wmod_loaded = sem("c_loaded"), sem("consts_loaded"), sem("wmod_loaded")
        x_loaded = [sem(f"x_loaded{b}") for b in range(NB)]
        silu_done, ones_ready = sem("silu_done"), sem("ones_ready")
        mod1_sums, mod1_ready, mod1_copied = sem("mod1_sums"), sem("mod1_ready"), sem("mod1_copied")
        mod2_loaded, mod2_sums, mod2_ready, mod2_steps = (
            sem(n) for n in ("mod2_loaded", "mod2_sums", "mod2_ready", "mod2_steps"))
        tables_loaded = sem("tables_loaded")
        w_loaded = [sem("w_loaded0"), sem("w_loaded1")]
        w_dequant, w_hi_done, w_lo_done = sem("w_dequant"), sem("w_hi_done"), sem("w_lo_done")
        k_proj, k_swapped, k_cos, k_sin, k_roped, k_hi_done, k_lo_done = (
            sem(n) for n in ("k_proj", "k_swapped", "k_cos", "k_sin", "k_roped", "k_hi_done", "k_lo_done"))
        v_proj, v_copied, v_turned, v_hi_done, v_lo_done = (
            sem(n) for n in ("v_proj", "v_copied", "v_turned", "v_hi_done", "v_lo_done"))
        q_proj, q_swapped, q_cos, q_sin, q_roped, q_hi_done, q_lo_done = (
            sem(n) for n in ("q_proj", "q_swapped", "q_cos", "q_sin", "q_roped", "q_hi_done", "q_lo_done"))
        scores_ready, max_ready, probs_ready = sem("scores_ready"), sem("max_ready"), sem("probs_ready")
        turn_ready, turn_hi, turn_lo = sem("turn_ready"), sem("turn_hi"), sem("turn_lo")
        recip_ready, r_stored, r_loaded = sem("recip_ready"), sem("r_stored"), sem("r_loaded")
        ctx_ready, ctx_scaled, ctx_hi_done, ctx_lo_done = (
            sem(n) for n in ("ctx_ready", "ctx_scaled", "ctx_hi_done", "ctx_lo_done"))
        out_ready, out_added = sem("out_ready"), sem("out_added")

        block = ctx.enter_context(nc.Block())

        PV_AT = (0, 2)
        OUT_AT = HPG + 1
        OUT_SLOTS = ((0, 1), (0, 2), (1, 0), (1, 1))

        def over_groups(eng, body):
            body(0, True, False)
            with eng.Fori(1, NKV - 1) as g:
                body(g, False, False)
            body(NKV - 1, False, True)

        JOBS_IN = ([], [], [JWO], [JWO + 1, JWO + 2], [JWO + 3, JWQ], [JWK, JWQ + 1], [JWV, JWQ + 2], [JWQ + 3])
        AHEAD = JWO

        def jobs_in(g, u, last):
            before = sum(len(x) for x in JOBS_IN[:u])
            jobs = []
            for i, k in enumerate(JOBS_IN[u]):
                if k >= JWO:
                    jobs.append((g, k, AHEAD + g * JOBS + before + i, (before + i) % 2))
                elif not last:
                    jobs.append((g + 1, k, AHEAD + g * JOBS + before + i, (before + i) % 2))
            return jobs

        def all_jobs(g, last):
            return [j for u in range(UNITS) for j in jobs_in(g, u, last)]

        def out_tile(g, u, t, first):
            if u == 0:
                return None if first else (1, t, g * ST - TPB + t, CTX)
            if (u - OUT_AT, t) in OUT_SLOTS:
                i = OUT_SLOTS.index((u - OUT_AT, t))
                return 0, i, g * ST + i, PROJ
            return None

        def q_quarters(u, t, last):
            if last and u + 2 >= UNITS:
                return []
            if u == OUT_AT:
                return {3: [0, 1, 2, 3]}.get(t, [])
            if u == OUT_AT + 1:
                return {2: [0, 1], 3: [2, 3]}.get(t, [])
            return {1: [0, 1], 2: [2], 3: [3]}.get(t, [])

        def ctx_split_slot(u):
            return (u + 2, 2) if u == HPG else (u + 2, 0)

        def w_parts(k):
            if k == JWK:
                hi, lo = wk_hi, wk_lo
            elif k == JWV:
                hi, lo = wv_hi, wv_lo
            elif k < JWO:
                hi, lo = wq_hi[k - JWQ], wq_lo[k - JWQ]
            else:
                return wo_hi[k - JWO][:, :], wo_lo[k - JWO][:, :]
            return hi[:, :, :].rearrange("p t n -> p (t n)"), lo[:, :, :].rearrange("p t n -> p (t n)")

        def turned_parts(n, j0, nj):
            b, t = n // (HPG * TPB), n % TPB
            at = j0 + TPB * (1 - b)
            return pT_hi[:, at:at + nj, t * P:(t + 1) * P], pT_lo[:, at:at + nj, t * P:(t + 1) * P]

        def chunk(bank, nj):
            return TURN[bank][:, 0:nj * P].rearrange("p (j q) -> p j q", q=P)

        KEYS, VALUES = [ps[:, 0, :], ps[:, 1, :]], [ps[:, 2, :], ps[:, 3, :]]
        VTURN = ps[:, 4:6, :].rearrange("p a n -> p (a n)")

        @block.sync
        def _(sp):
            def load_job(g, k, slot):
                sp.dma_start(w_int[:, slot, :], wjobs[g, k]).then_inc(w_loaded[slot], 16)
                sp.dma_start(w_scale[:, slot, :], sjobs[g, k].partition_broadcast(P)).then_inc(w_loaded[slot], 16)

            def spread_recip(g, u, loads):
                sp.wait_ge(recip_ready, g * UNITS + u + 1)
                sp.dma_start(r_scratch[u % 2].rearrange("(t p) -> p t", p=P), row_recip[:, u % 2, :],
                             allow_slow_non_contiguous=True).then_inc(r_stored, 16)
                for job in loads:
                    load_job(*job)
                sp.wait_ge(r_stored, (g * UNITS + u + 1) * 16)
                sp.dma_start(r_spread[:, u % 2, :], r_scratch[u % 2].partition_broadcast(P)).then_inc(r_loaded, 16)

            def load_x(b, loaded):
                sp.dma_start(x[:, b * TPB:(b + 1) * TPB, :],
                             x_dram[b * QB:(b + 1) * QB, :].rearrange("(t p) n -> p t n", p=P)).then_inc(loaded[b], 16)

            def load_mod2(j):
                col, places, _ = MOD2[j]
                for kt in range(KT):
                    sp.dma_start(places[kt][:, :], wmod_dram[kt * P:(kt + 1) * P, col * H:(col + 1) * H])\
                        .then_inc(mod2_loaded, 16)

            sp.dma_start(c_col[:, :], c_dram).then_inc(c_loaded, 16)
            load_x(0, x_loaded)
            for j, w in enumerate((w_shift, w_scale1)):
                sp.dma_start(w[:, :, :], wmod_dram[:, j * H:(j + 1) * H].rearrange("(t p) n -> p t n", p=P))\
                    .then_inc(wmod_loaded, 16)
            sp.dma_start(ident[:, :], ident_dram).then_inc(consts_loaded, 16)
            load_job(0, 0, 0)
            load_x(1, x_loaded)
            sp.dma_start(masks[:, :, :], masks_dram).then_inc(consts_loaded, 16)
            for k in range(1, AHEAD):
                if k >= 2:
                    sp.wait_ge(w_dequant, k - 1)
                load_job(0, k, k % 2)
                if k == 1:
                    sp.dma_start(cosT[:, :], cos_dram).then_inc(tables_loaded, 16)
                    sp.dma_start(sinT[:, :], sin_dram).then_inc(tables_loaded, 16)
            for g, k, number, slot in all_jobs(0, False)[:2]:
                sp.wait_ge(w_dequant, number - 1)
                load_job(g, k, slot)

            def body(g, first, last):
                jobs = [(x[0], x[1]) for x in all_jobs(g, last)[2:]]
                if not last:
                    jobs += [(g + 1, JWO), (g + 1, JWO + 1)]
                for u in range(UNITS):
                    done = jobs_in(g, u, last)
                    loads = [(*jobs.pop(0), x[3]) for x in done if jobs]
                    spread_recip(g, u, loads)
                    if last and u in MOD2_LOAD:
                        j = MOD2_LOAD.index(u)
                        if j == 0:
                            sp.wait_ge(v_proj, NKV * NB)
                        elif j == 1:
                            sp.wait_ge(mod2_sums, KT)
                        else:
                            sp.wait_ge(q_proj, g * UNITS + HPG + 2 * (j - 1))
                        load_mod2(j)
                if last:
                    sp.wait_ge(ctx_ready, NKV * UNITS)
                    for b in range(NB):
                        load_x(b, x_again)
            over_groups(sp, body)

        @block.gpsimd
        def _(pool):
            pool.memset(ones[:, :], 1.0).then_inc(ones_ready, 1)

            def w_lo(number, k, slot):
                hi, lo = w_parts(k)
                pool.wait_ge(w_hi_done, number + 1)
                pool.tensor_tensor(lo, w_full[:, slot, :], f32(hi), ALU.subtract).then_inc(w_lo_done, 1)

            def q_add(unit):
                pool.wait_ge(q_sin, unit + 1)
                pool.tensor_tensor(roped[:, :], cosed[:, :], sined[:, :], ALU.add).then_inc(q_roped, 1)

            def ctx_lo_part(g, u):
                pool.wait_ge(ctx_hi_done, g * UNITS + u + 1)
                pool.tensor_tensor(ctx_lo[:, u % HPG, :], ctx_full[:, :], f32(ctx_hi[:, u % HPG, :]),
                                   ALU.subtract).then_inc(ctx_lo_done, 1)

            w_lo(0, 0, 0)
            for n in range(KT):
                norm.piece_lo(pool, n)
            w_lo(1, 1, 1)
            for n in range(KT, NB * KT):
                norm.piece_lo(pool, n)
            pool.memset(f32(pT_hi[:, 5, 0:P]), 0.0)
            pool.memset(f32(pT_lo[:, 5, 0:P]), 0.0)
            pool.memset(f32(pT_hi[:, 7, 2 * P:3 * P]), 0.0)
            pool.memset(f32(pT_lo[:, 7, 2 * P:3 * P]), 0.0).then_inc(ctx_lo_done, 1)
            for k in range(2, AHEAD):
                w_lo(k, k, k % 2)
            q_add(0)
            pool.memset(acc[:, :, :], 0.0).then_inc(out_added, 1)

            def body(g, first, last):
                for u in range(UNITS):
                    if not (last and u == UNITS - 1):
                        if not (isinstance(g, int) and g == 0 and u == 0):
                            pool.wait_ge(q_lo_done, g * UNITS + u + 1)
                        else:
                            pool.wait_ge(q_lo_done, 1)
                        q_add(g * UNITS + u + 1)
                    for w in range(UNITS):
                        if ctx_split_slot(w)[0] == u:
                            ctx_lo_part(g, w)
                    for _, k, number, slot in jobs_in(g, u, last):
                        w_lo(number, k, slot)
                ctx_lo_part(g, UNITS - 2)
            over_groups(pool, body)

        @block.scalar
        def _(act):
            def w_hi(number, k, slot):
                act.wait_ge(w_dequant, number + 1)
                act.copy(w_parts(k)[0], w_full[:, slot, :]).then_inc(w_hi_done, 1)

            def swap_halves(src):
                act.copy(swapped[0:64, :], src[64:128, :])
                return act.copy(swapped[64:128, :], src[0:64, :])

            def q_swap(unit, src):
                act.wait_ge(q_proj, unit + 1)
                swap_halves(src).then_inc(q_swapped, 1)

            def q_hi(unit, u):
                act.wait_ge(q_roped, unit + 1)
                act.copy(qT_hi[:, u % 2, :], roped[:, :]).then_inc(q_hi_done, 1)

            def turn(g, n):
                for c, j0, nj in chunks_of(n):
                    act.wait_ge(turn_ready, g * CHUNKS + c + 1)
                    act.copy(turned_parts(n, j0, nj)[0], chunk(c % 2, nj)).then_inc(turn_hi, 1)

            def ctx_hi_part(g, u):
                act.wait_ge(ctx_scaled, g * UNITS + u + 1)
                if u == HPG:
                    act.wait_ge(out_ready, g * ST + TPB)
                act.copy(ctx_hi[:, u % HPG, :], ctx_full[:, :]).then_inc(ctx_hi_done, 1)

            def k_swap(g, half):
                act.wait_ge(k_proj, g * NB + half + 1)
                if half:
                    act.wait_ge(k_sin, g * NB + half)
                swap_halves(KEYS[half]).then_inc(k_swapped, 1)

            def k_hi(g, half):
                act.wait_ge(k_roped, g * NB + half + 1)
                act.copy(kT_hi[:, half * QB:(half + 1) * QB], roped_k[:, half, :]).then_inc(k_hi_done, 1)

            def v_copy(g, half):
                act.wait_ge(v_proj, g * NB + half + 1)
                act.copy(vT[:, half * QB:(half + 1) * QB], VALUES[half]).then_inc(v_copied, 1)

            def v_hi_part(g):
                act.wait_ge(v_turned, g + 1)
                act.copy(v_hi[:, :, :].rearrange("p t d -> p (t d)"), VTURN).then_inc(v_hi_done, 1)

            act.wait_ge(c_loaded, 16)
            act.activation(c_silu[:, :], c_col[:, :], ACT.Silu).then_inc(silu_done, 1)
            norm.root_act(act, 0)
            w_hi(0, 0, 0)
            act.wait_ge(mod1_copied, 2)
            for n in range(KT):
                if n == 2:
                    norm.root_act(act, 1)
                norm.piece_act(act, n)
            w_hi(1, 1, 1)
            norm.piece_act(act, KT)
            norm.piece_act(act, KT + 1)
            w_hi(2, 2, 0)
            norm.piece_act(act, KT + 2)
            norm.piece_act(act, KT + 3)
            w_hi(3, 3, 1)
            k_swap(0, 0)
            k_hi(0, 0)
            k_swap(0, 1)
            w_hi(4, 4, 0)
            k_hi(0, 1)
            w_hi(5, 5, 1)
            v_copy(0, 0)
            v_copy(0, 1)
            q_swap(0, CTX)
            v_hi_part(0)
            q_hi(0, 0)

            def body(g, first, last):
                for n in range(TILES):
                    u, t = n // TPB, n % TPB
                    width = (u // HPG * TPB + t + 1) * P
                    more = not (last and u == UNITS - 1)
                    if t == 0 and more:
                        q_swap(g * UNITS + u + 1, PROJ)
                    if n >= 2:
                        turn(g, n - 2)
                    act.wait_ge(max_ready, g * TILES + n + 1)
                    act.activation(probs[:, n % 2, 0:width], SCORES[n % 2][:, 0:width], ACT.Exp,
                                   bias=neg_max[:, n % 2:n % 2 + 1], scale=-1.0,
                                   accum_out=row_sum[:, u % 2, t:t + 1]).then_inc(probs_ready, 1)
                    if t == 1 and more:
                        q_hi(g * UNITS + u + 1, u + 1)
                    for w in range(UNITS):
                        if ctx_split_slot(w) == (u, t):
                            ctx_hi_part(g, w)
                    jobs = jobs_in(g, u, last)
                    if 2 <= t < 2 + len(jobs):
                        _, k, number, slot = jobs[t - 2]
                        w_hi(number, k, slot)
                ctx_hi_part(g, UNITS - 2)
                if not last:
                    k_swap(g + 1, 0)
                    k_swap(g + 1, 1)
                turn(g, TILES - 2)
                if not last:
                    k_hi(g + 1, 0)
                    v_copy(g + 1, 0)
                turn(g, TILES - 1)
                if not last:
                    k_hi(g + 1, 1)
                    v_copy(g + 1, 1)
                ctx_hi_part(g, UNITS - 1)
                if not last:
                    v_hi_part(g + 1)
            over_groups(act, body)

        @block.vector
        def _(dve):
            def dequant(g, k, number, slot, count):
                dve.wait_ge(w_loaded[slot], count * 32)
                if not (isinstance(number, int) and number < 2):
                    dve.wait_ge(w_lo_done, number - 1)
                dve.scalar_tensor_tensor(out=w_full[:, slot, :], in0=w_int[:, slot, :], scalar=-ZERO,
                                         in1=w_scale[:, slot, :], op0=ALU.add, op1=ALU.mult).then_inc(w_dequant, 1)

            def q_rope(unit, u, src, first=False):
                c = slice(u // HPG * QB, (u // HPG + 1) * QB)
                dve.wait_ge(q_swapped, unit + 1)
                if not first:
                    dve.wait_ge(q_roped, unit)
                dve.scalar_tensor_tensor(out=cosed[:, :], in0=src, scalar=-SCALE, in1=cosT[:, c],
                                         op0=ALU.mult, op1=ALU.mult).then_inc(q_cos, 1)
                dve.scalar_tensor_tensor(out=sined[:, :], in0=swapped[:, :], scalar=-SCALE, in1=sinT[:, c],
                                         op0=ALU.mult, op1=ALU.mult).then_inc(q_sin, 1)

            def q_lo_part(unit, u):
                dve.wait_ge(q_hi_done, unit + 1)
                dve.tensor_tensor(qT_lo[:, u % 2, :], roped[:, :], f32(qT_hi[:, u % 2, :]),
                                  ALU.subtract).then_inc(q_lo_done, 1)

            def k_rope(g, half):
                c = slice(half * QB, (half + 1) * QB)
                i = g * NB + half + 1
                dve.wait_ge(k_swapped, i)
                dve.tensor_tensor(roped_k[:, half, :], KEYS[half], cosT[:, c], ALU.mult).then_inc(k_cos, 1)
                if not isinstance(g, int) or g:
                    dve.wait_ge(q_roped, g * UNITS + 1)
                dve.tensor_tensor(sined[:, :], swapped[:, :], sinT[:, c], ALU.mult).then_inc(k_sin, 1)
                dve.wait_ge(k_cos, i)
                dve.wait_ge(k_sin, i)
                dve.tensor_tensor(roped_k[:, half, :], roped_k[:, half, :], sined[:, :], ALU.add).then_inc(k_roped, 1)
                dve.wait_ge(k_roped, i)

            def k_lo_part(g, half):
                c = slice(half * QB, (half + 1) * QB)
                dve.wait_ge(k_hi_done, g * NB + half + 1)
                dve.tensor_tensor(kT_lo[:, c], roped_k[:, half, :], f32(kT_hi[:, c]), ALU.subtract).then_inc(k_lo_done, 1)

            def v_lo_part(g):
                dve.wait_ge(v_hi_done, g + 1)
                dve.tensor_tensor(v_lo[:, :, :].rearrange("p t d -> p (t d)"), VTURN,
                                  f32(v_hi[:, :, :].rearrange("p t d -> p (t d)")), ALU.subtract).then_inc(v_lo_done, 1)

            def turn(g, n):
                for c, j0, nj in chunks_of(n):
                    hi, lo = turned_parts(n, j0, nj)
                    dve.wait_ge(turn_hi, g * CHUNKS + c + 1)
                    dve.tensor_tensor(lo, chunk(c % 2, nj), f32(hi), ALU.subtract).then_inc(turn_lo, 1)

            def recip(g, u):
                dve.wait_ge(probs_ready, g * TILES + (u + 1) * TPB)
                dve.reciprocal(row_recip[:, u % 2, :], row_sum[:, u % 2, :]).then_inc(recip_ready, 1)

            def ctx_scale(g, u):
                dve.wait_ge(ctx_ready, g * UNITS + u + 1)
                dve.wait_ge(r_loaded, (g * UNITS + u + 1) * 16)
                dve.wait_ge(ctx_lo_done, g * UNITS + u + 1)
                dve.tensor_tensor(ctx_full[:, :], CTX, r_spread[:, u % 2, :], ALU.mult).then_inc(ctx_scaled, 1)

            def out_add(number, tile, src):
                dve.wait_ge(out_ready, number + 1)
                dve.tensor_tensor(acc[:, tile, :], src, acc[:, tile, :], ALU.add).then_inc(out_added, 1)

            def weigh(rows, kt, total, sums, count):
                if kt == 0:
                    dve.tensor_scalar(total, rows, c_silu[:, kt:kt + 1], None, ALU.mult).then_inc(sums, 1)
                else:
                    dve.wait_ge(sums, count)
                    dve.scalar_tensor_tensor(out=total, in0=rows, scalar=c_silu[:, kt:kt + 1], in1=total,
                                             op0=ALU.mult, op1=ALU.add).then_inc(sums, 1)

            def mod2_sum(j, kt):
                _, places, total = MOD2[j]
                dve.wait_ge(mod2_loaded, 16 * (j + 1) * KT)
                weigh(places[kt][:, :], kt, total, mod2_sums, j * KT + kt)

            def mod2_columns():
                gates, rest = slice(0, 2 * KT), slice(2 * KT, 3 * KT)
                dve.wait_ge(mod2_ready, 1)
                dve.tensor_scalar(mod_sign[:, :], PROJ[:, gates], 0.0, 2.0, ALU.is_ge, ALU.mult).then_inc(mod2_steps, 1)
                dve.tensor_scalar(mod_mag[:, :], PROJ[:, gates], -1.0, None, ALU.mult).then_inc(mod2_steps, 1)
                dve.tensor_copy(mod_cols[:, rest], PROJ[:, rest]).then_inc(mod2_steps, 1)
                dve.tensor_scalar(mod_cols[:, 3 * KT:4 * KT], PROJ[:, 3 * KT:4 * KT], 1.0, None,
                                  ALU.add).then_inc(mod2_steps, 1)
                dve.wait_ge(mod2_steps, 4)
                dve.tensor_tensor(mod_mag[:, :], mod_mag[:, :], PROJ[:, gates], ALU.max).then_inc(mod2_steps, 1)
                dve.wait_ge(mod2_steps, 5)
                dve.tensor_scalar(mod_mag[:, :], mod_mag[:, :], 0.25, None, ALU.max).then_inc(mod2_steps, 1)
                dve.wait_ge(mod2_steps, 6)
                dve.scalar_tensor_tensor(out=mod_cols[:, gates], in0=mod_sign[:, :], scalar=-1.0, in1=mod_mag[:, :],
                                         op0=ALU.add, op1=ALU.mult).then_inc(mod2_steps, 1)

            dve.wait_ge(x_loaded[0], 16)
            norm.tokens_dve(dve, 0)
            dequant(0, 0, 0, 0, 1)
            dve.wait_ge(silu_done, 1)
            dve.wait_ge(wmod_loaded, 32)
            for kt in range(KT):
                for j, w in enumerate((w_shift, w_scale1)):
                    weigh(w[:, kt, :], kt, mod1_rows[:, j, :], mod1_sums, 2 * kt + j - 1)
            dve.wait_ge(mod1_ready, 1)
            dve.tensor_copy(mod1[:, 0:KT], CTX[:, 0:KT]).then_inc(mod1_copied, 1)
            dve.tensor_scalar(mod1[:, KT:2 * KT], CTX[:, KT:2 * KT], 1.0, None, ALU.add).then_inc(mod1_copied, 1)
            dve.wait_ge(x_loaded[1], 16)
            norm.tokens_dve(dve, 1)
            for k in (1, 2, 3):
                dequant(0, k, k, k % 2, k // 2 + 1)
            dve.wait_ge(tables_loaded, 32)
            k_rope(0, 0)
            k_lo_part(0, 0)
            dequant(0, 4, 4, 0, 3)
            k_rope(0, 1)
            k_lo_part(0, 1)
            dequant(0, 5, 5, 1, 3)
            q_rope(0, 0, CTX, first=True)
            v_lo_part(0)
            q_lo_part(0, 0)

            def body(g, first, last):
                pending = None
                for n in range(TILES):
                    u, t = n // TPB, n % TPB
                    width = (u // HPG * TPB + t + 1) * P
                    more = not (last and u == UNITS - 1)
                    if t == 0 and u:
                        recip(g, u - 1)
                    dve.wait_ge(scores_ready, g * TILES + n + 1)
                    dve.tensor_reduce(neg_max[:, n % 2:n % 2 + 1], SCORES[n % 2][:, 0:width], AX.X,
                                      ALU.min).then_inc(max_ready, 1)
                    if pending is not None:
                        b, i, number, bank = pending
                        if first and number == 0:
                            dve.wait_ge(out_added, 1)
                        out_add(number, b * TPB + i, bank)
                    pending = out_tile(g, u, t, first)
                    if t == 0 and more:
                        q_rope(g * UNITS + u + 1, (u + 1) % UNITS, PROJ)
                    if t == 2 and more:
                        q_lo_part(g * UNITS + u + 1, u + 1)
                    jobs = jobs_in(g, u, last)
                    if 1 <= t < 1 + len(jobs):
                        gj, k, number, slot = jobs[t - 1]
                        before = sum(len(x) for x in JOBS_IN[:u]) + t - 1
                        dequant(gj, k, number, slot, AHEAD // 2 + g * (JOBS // 2) + before // 2 + 1)
                    if t == 3 and u:
                        ctx_scale(g, u - 1)
                    if last and u in MOD2_SUM:
                        mod2_sum(MOD2_SUM.index(u), t)
                    if n >= 2:
                        turn(g, n - 2)
                recip(g, UNITS - 1)
                if not last:
                    k_rope(g + 1, 0)
                turn(g, TILES - 2)
                if not last:
                    k_rope(g + 1, 1)
                    k_lo_part(g + 1, 0)
                turn(g, TILES - 1)
                if not last:
                    k_lo_part(g + 1, 1)
                if last:
                    mod2_columns()
                ctx_scale(g, UNITS - 1)
                dve.wait_ge(ctx_hi_done, (g + 1) * UNITS)
                dve.tensor_tensor(ctx_lo[:, HPG - 1, :], ctx_full[:, :], f32(ctx_hi[:, HPG - 1, :]),
                                  ALU.subtract).then_inc(ctx_lo_done, 1)
                if not last:
                    v_lo_part(g + 1)
                else:
                    for i in range(TPB):
                        out_add(NKV * ST - TPB + i, TPB + i, ps[:, i, :])
            over_groups(dve, body)

        @block.tensor
        def _(pe):
            def projected(out, w_hi, w_lo, b, tiles=range(KT)):
                c = slice(b * QB, (b + 1) * QB)
                for kt in tiles:
                    pe.matmul(out, w_hi[:, kt, :], hT_hi[:, kt, c], start=(kt == 0), stop=False)
                    pe.matmul(out, w_hi[:, kt, :], hT_lo[:, kt, c], start=False, stop=False)
                    mm = pe.matmul(out, w_lo[:, kt, :], hT_hi[:, kt, c], start=False, stop=(kt == KT - 1))
                return mm

            def scores(g, n):
                u, t = n // TPB, n % TPB
                i = (u // HPG) * TPB + t
                out = SCORES[n % 2]
                if t == 0:
                    pe.wait_ge(q_lo_done, g * UNITS + u + 1)
                if n == 0:
                    pe.wait_ge(k_lo_done, (g + 1) * NB)
                elif n >= 2:
                    pe.wait_ge(probs_ready, g * TILES + n - 1)
                width = (i + 1) * P
                q = slice(t * P, (t + 1) * P)
                for c0 in range(0, width, 512):
                    c = slice(c0, c0 + max(NSMALL, min(512, width - c0)))
                    pe.matmul(out[:, c], qT_hi[:, u % 2, q], kT_hi[:, c], start=True, stop=False)
                    pe.matmul(out[:, c], qT_hi[:, u % 2, q], kT_lo[:, c], start=False, stop=False)
                    pe.matmul(out[:, c], qT_lo[:, u % 2, q], kT_hi[:, c], start=False, stop=(c0 + 512 < width))
                pe.matmul(out[:, i * P:(i + 1) * P], identb, maskb, start=False, stop=True).then_inc(scores_ready, 1)

            def turn(g, n):
                pe.wait_ge(probs_ready, g * TILES + n + 1)
                for c, j0, nj in chunks_of(n):
                    if c >= 2:
                        pe.wait_ge(turn_lo, g * CHUNKS + c - 1)
                    else:
                        pe.wait_ge(v_lo_done, g + 1)
                    for j in range(nj):
                        mm = pe.transpose(TURN[c % 2][:, j * P:(j + 1) * P],
                                          probs[:, n % 2, (j0 + j) * P:(j0 + j + 1) * P], ident[:, :])
                    mm.then_inc(turn_ready, 1)

            def times_v(g, u, side):
                b = u // HPG
                last_chunk = chunks_of(u * TPB + 2 * side + 1)[-1][0]
                pe.wait_ge(turn_lo, g * CHUNKS + last_chunk + 1)
                if u == 0 and side == 0:
                    pe.wait_ge(out_added, 1 + g * ST)
                elif side == 0:
                    pe.wait_ge(ctx_scaled, g * UNITS + u)
                c = slice(side * 2 * P, (side + 1) * 2 * P)
                tiles = b * TPB + 2 * side + 2
                for j in range(tiles):
                    at = j + TPB * (1 - b)
                    pe.matmul(CTX[:, c], v_hi[:, j, :], pT_hi[:, at, c], start=(j == 0), stop=False)
                    pe.matmul(CTX[:, c], v_hi[:, j, :], pT_lo[:, at, c], start=False, stop=False)
                    mm = pe.matmul(CTX[:, c], v_lo[:, j, :], pT_hi[:, at, c], start=False, stop=(j == tiles - 1))
                if side == 1:
                    mm.then_inc(ctx_ready, 1)

            def project_out(tt, out):
                q = slice(tt * P, (tt + 1) * P)
                for h in range(HPG):
                    pe.matmul(out, ctx_hi[:, h, q], wo_hi[h][:, :], start=(h == 0), stop=False)
                    pe.matmul(out, ctx_hi[:, h, q], wo_lo[h][:, :], start=False, stop=False)
                    mm = pe.matmul(out, ctx_lo[:, h, q], wo_hi[h][:, :], start=False, stop=(h == HPG - 1))
                mm.then_inc(out_ready, 1)

            def keys(g):
                for half in range(NB):
                    projected(KEYS[half], wk_hi, wk_lo, half).then_inc(k_proj, 1)

            def values(g, half):
                if half == 0 and not (isinstance(g, int) and g == 0):
                    pe.wait_ge(probs_ready, g * TILES)
                projected(VALUES[half], wv_hi, wv_lo, half).then_inc(v_proj, 1)

            def turn_values(g):
                pe.wait_ge(v_copied, (g + 1) * NB)
                for j in range(ST):
                    mm = pe.transpose(VTURN[:, j * P:(j + 1) * P], vT[:, j * P:(j + 1) * P], ident[:, :])
                mm.then_inc(v_turned, 1)

            def mod_columns(out, sums, ready):
                for j, rows in enumerate(sums):
                    for kt in range(KT):
                        mm = pe.matmul(out[:, j * KT + kt:j * KT + kt + 1], rows[:, kt * P:(kt + 1) * P], ones[:, :],
                                       start=True, stop=True)
                mm.then_inc(ready, 1)

            pe.wait_ge(ones_ready, 1)
            pe.wait_ge(mod1_sums, 2 * KT)
            mod_columns(CTX, [mod1_rows[:, j, :] for j in range(2)], mod1_ready)
            pe.wait_ge(consts_loaded, 32)
            for n in range(KT + 2):
                norm.piece_pe(pe, n)
            pe.wait_ge(w_lo_done, 1)
            pe.wait_ge(norm.lo_done, KT)
            projected(KEYS[0], wk_hi, wk_lo, 0).then_inc(k_proj, 1)
            for n in range(KT + 2, NB * KT):
                norm.piece_pe(pe, n)
            pe.wait_ge(norm.lo_done, NB * KT)
            projected(KEYS[1], wk_hi, wk_lo, 1).then_inc(k_proj, 1)
            pe.wait_ge(w_lo_done, 2)
            values(0, 0)
            values(0, 1)
            pe.wait_ge(w_lo_done, 3)
            projected(CTX, wq_hi[0], wq_lo[0], 0).then_inc(q_proj, 1)
            pe.wait_ge(w_lo_done, 4)
            projected(PROJ, wq_hi[1], wq_lo[1], 0).then_inc(q_proj, 1)
            turn_values(0)
            pe.wait_ge(w_lo_done, AHEAD)
            pe.wait_ge(ctx_lo_done, 1)
            scores(0, 0)

            def body(g, first, last):
                for n in range(TILES):
                    u, t = n // TPB, n % TPB
                    if n + 1 < TILES:
                        scores(g, n + 1)
                    elif not last:
                        pe.wait_ge(probs_ready, g * TILES + n)
                        keys(g + 1)
                    if u and t in PV_AT:
                        times_v(g, u - 1, PV_AT.index(t))
                    tile = out_tile(g, u, t, first)
                    if tile is not None:
                        b, i, number, bank = tile
                        if i == 0:
                            pe.wait_ge(ctx_lo_done, 1 + (g * UNITS + HPG if b == 0 else g * UNITS))
                        if b == 0 and i in (0, 2):
                            pe.wait_ge(q_cos, g * UNITS + u + 2)
                        elif i:
                            pe.wait_ge(out_added, 1 + number)
                        project_out(i, bank)
                    quarters = q_quarters(u, t, last)
                    if quarters:
                        w = (u + 2) % UNITS
                        if quarters[0] == 0:
                            if u in (OUT_AT, OUT_AT + 1):
                                pe.wait_ge(out_added, 1 + g * ST + 2 * (u - OUT_AT + 1))
                            else:
                                pe.wait_ge(q_cos, g * UNITS + u + 2)
                            if u + 2 >= UNITS:
                                k = JWQ + w % HPG
                                number = [x[2] for x in all_jobs(g, last) if x[1] == k][0]
                                pe.wait_ge(w_lo_done, number + 1)
                        mm = projected(PROJ, wq_hi[w % HPG], wq_lo[w % HPG], w // HPG, quarters)
                        if quarters[-1] == KT - 1:
                            mm.then_inc(q_proj, 1)
                    if n:
                        turn(g, n - 1)
                if not last:
                    values(g + 1, 0)
                turn(g, TILES - 1)
                if last:
                    pe.wait_ge(mod2_sums, len(MOD2) * KT)
                    pe.wait_ge(out_added, 1 + g * ST + TPB)
                    mod_columns(PROJ, [total for _, _, total in MOD2], mod2_ready)
                times_v(g, UNITS - 1, 0)
                if not last:
                    values(g + 1, 1)
                times_v(g, UNITS - 1, 1)
                if not last:
                    pe.wait_ge(turn_lo, (g + 1) * CHUNKS)
                    turn_values(g + 1)
                    scores(g + 1, 0)
                else:
                    pe.wait_ge(ctx_lo_done, 1 + NKV * UNITS)
                    for i in range(TPB):
                        project_out(i, ps[:, i, :])
            over_groups(pe, body)


def residual_phase(nc, acc, x, x_loaded, mod_cols, gates, ident, hT_hi, hT_lo, raw, raw_loaded, ffn_dram):
    ctx = ExitStack()
    with ctx:
        al = Allocator(nc, ctx)
        xn, z = al.sbuf("n2_xn", [P, ST, H]), al.sbuf("n2_z", [P, 2, QB])
        ps = al.psum("n2_ps", [P, 4, 512])
        norm = Normalise(nc, al, "n2_", acc, xn, z, [ps[:, 0, :], ps[:, 1, :]], mod_cols[:, 2 * KT:3 * KT],
                         mod_cols[:, 3 * KT:4 * KT], ident, hT_hi, hT_lo)
        gate_ready, gate_copied, scaled, added = (al.sem(n) for n in ("gate_ready", "gate_copied", "r_scaled", "r_added"))
        block = ctx.enter_context(nc.Block())

        @block.sync
        def _(sp):
            for s in range(2):
                sp.dma_start(raw[:, s, :], ffn_dram[s]).then_inc(raw_loaded[s], 16)

        @block.tensor
        def _(pe):
            for j in range(2):
                for kt in range(KT):
                    col = mod_cols[:, j * KT + kt:j * KT + kt + 1]
                    mm = pe.matmul(ps[:, 2 + j, kt * P:(kt + 1) * P], col.to_broadcast([P, P]), ident[:, :],
                                   start=True, stop=True)
                mm.then_inc(gate_ready, 1)
            for n in range(NB * KT):
                norm.piece_pe(pe, n)

        @block.scalar
        def _(act):
            for j in range(2):
                act.wait_ge(gate_ready, j + 1)
                act.copy(gates[:, j, :], ps[:, 2 + j, :]).then_inc(gate_copied, 1)
            norm.root_act(act, 0)
            for n in range(KT):
                norm.piece_act(act, n)
            norm.root_act(act, 1)
            for n in range(KT, NB * KT):
                norm.piece_act(act, n)

        @block.vector
        def _(dve):
            dve.wait_ge(gate_copied, 1)
            for b in range(NB):
                for i in range(b * TPB, (b + 1) * TPB):
                    dve.tensor_tensor(acc[:, i, :], acc[:, i, :], gates[:, 0, :], ALU.mult).then_inc(scaled, 1)
                dve.wait_ge(x_loaded[b], 16)
                for i in range(b * TPB, (b + 1) * TPB):
                    dve.wait_ge(scaled, i + 1)
                    dve.tensor_tensor(acc[:, i, :], acc[:, i, :], x[:, i, :], ALU.add).then_inc(added, 1)
                dve.wait_ge(added, (b + 1) * TPB)
                norm.tokens_dve(dve, b)

        @block.gpsimd
        def _(pool):
            for n in range(NB * KT):
                norm.piece_lo(pool, n)


def ffn_phase(nc, hT_hi, hT_lo, x, gate, raw, loaded, ffn_dram, out_dram):
    ctx = ExitStack()
    with ctx:
        al = Allocator(nc, ctx)
        sbuf, psum, sem = al.sbuf, al.psum, (lambda n: al.sem("ffn_" + n))
        w_gu = [sbuf(f"ffn_w_gu{s}", [P, 2 * KT, P], F32R) for s in range(2)]
        w_down = [sbuf(f"ffn_w_down{s}", [P, H], F32R) for s in range(2)]
        gated, mid = sbuf("ffn_gated", [P, 2, QB]), sbuf("ffn_mid", [P, 2, QB])
        mid_hi = [sbuf(f"ffn_mid_hi{s}", [P, QB], F32R) for s in range(2)]
        mid_lo = [sbuf(f"ffn_mid_lo{s}", [P, QB], F32R) for s in range(2)]
        fin = sbuf("ffn_fin", [P, TPB, H])
        ps = psum("ffn_ps", [P, 8, 512])
        gu_cast, down_cast, gate_up, silued, product, hi_done, lo_done, down = (
            sem(n) for n in ("gu_cast", "down_cast", "gate_up", "silued", "product", "hi_done", "lo_done", "down"))
        scaled, added, stored = sem("scaled"), sem("added"), sem("stored")
        block = ctx.enter_context(nc.Block())
        PAIRS = MT // 2

        def over_steps(eng, body, first=0, after=None):
            for b in range(NB):
                for i in range(first):
                    for s in range(2):
                        body(b, i, s)
                with eng.Fori(first, PAIRS - 1) as i:
                    for s in range(2):
                        body(b, i, s)
                for s in range(2):
                    body(b, PAIRS - 1, s)
                if after is not None:
                    after(b)

        @block.sync
        def _(sp):
            def body(b, i, s):
                if isinstance(i, int):
                    if b == NB - 1:
                        return
                    i_next = 0
                else:
                    i_next = i + 1
                sp.wait_ge(down_cast, b * MT + i * 2 + s + 1)
                sp.dma_start(raw[:, s, :], ffn_dram[i_next * 2 + s]).then_inc(loaded[s], 16)
            over_steps(sp, body)
            for i in range(ST):
                sp.wait_ge(added, i + 1)
                sp.dma_start(out_dram[i * P:(i + 1) * P, :], x[:, i, :]).then_inc(stored, 16)
            sp.wait_ge(stored, 16 * ST)

        @block.scalar
        def _(act):
            def body(b, i, s):
                m = b * MT + i * 2 + s
                act.wait_ge(gate_up, m + 1)
                act.activation(gated[:, s, :], ps[:, 2 * s, :], ACT.Silu).then_inc(silued, 1)
                act.wait_ge(product, m + 1)
                act.copy(mid_hi[s][:, :], mid[:, s, :]).then_inc(hi_done, 1)
            over_steps(act, body)

        @block.vector
        def _(dve):
            def cast_gu(count, s):
                dve.wait_ge(loaded[s], count * 16)
                dve.tensor_copy(w_gu[s][:, :, :].rearrange("p a n -> p (a n)"), raw[:, s, 0:2 * H]).then_inc(gu_cast, 1)

            def cast_down(s):
                dve.tensor_copy(w_down[s][:, :], raw[:, s, 2 * H:3 * H]).then_inc(down_cast, 1)

            def body(b, i, s):
                m = b * MT + i * 2 + s
                end = isinstance(i, int) and i == PAIRS - 1 and b == NB - 1
                dve.wait_ge(silued, m + 1)
                dve.tensor_tensor(mid[:, s, :], gated[:, s, :], ps[:, 2 * s + 1, :], ALU.mult).then_inc(product, 1)
                if not end:
                    cast_gu(b * PAIRS + i + 2, s)
                if not (end and s == 1):
                    if not (isinstance(m, int) and m == 0):
                        dve.wait_ge(down, m)
                    cast_down(1 - s)
                dve.wait_ge(hi_done, m + 1)
                dve.tensor_tensor(mid_lo[s][:, :], mid[:, s, :], f32(mid_hi[s][:, :]), ALU.subtract).then_inc(lo_done, 1)

            def after(b):
                dve.wait_ge(down, (b + 1) * MT)
                for t in range(TPB):
                    i = b * TPB + t
                    dve.tensor_tensor(fin[:, t, :], ps[:, 4 + t, :], gate, ALU.mult).then_inc(scaled, 1)
                    dve.wait_ge(scaled, i + 1)
                    dve.tensor_tensor(x[:, i, :], x[:, i, :], fin[:, t, :], ALU.add).then_inc(added, 1)

            cast_gu(1, 0)
            cast_gu(1, 1)
            cast_down(0)
            over_steps(dve, body, first=1, after=after)

        @block.tensor
        def _(pe):
            def project(b, i, s):
                m = b * MT + i * 2 + s
                pe.wait_ge(gu_cast, m + 1)
                if not (isinstance(i, int) and i == 0 and b == 0):
                    pe.wait_ge(product, m - 1)
                c = slice(b * QB, (b + 1) * QB)
                for a in range(2):
                    for kt in range(KT):
                        pe.matmul(ps[:, 2 * s + a, :], w_gu[s][:, a * KT + kt, :], hT_hi[:, kt, c],
                                  start=(kt == 0), stop=False)
                        mm = pe.matmul(ps[:, 2 * s + a, :], w_gu[s][:, a * KT + kt, :], hT_lo[:, kt, c],
                                       start=False, stop=(kt == KT - 1))
                mm.then_inc(gate_up, 1)

            def project_down(m, s, first=False, last=False):
                pe.wait_ge(lo_done, m + 1)
                for t in range(TPB):
                    q = slice(t * P, (t + 1) * P)
                    pe.matmul(ps[:, 4 + t, :], mid_hi[s][:, q], w_down[s][:, :], start=first, stop=False)
                    mm = pe.matmul(ps[:, 4 + t, :], mid_lo[s][:, q], w_down[s][:, :], start=False, stop=last)
                mm.then_inc(down, 1)

            def body(b, i, s):
                project(b, i, s)
                m = b * MT + i * 2 + s
                if isinstance(i, int) and i == 0 and s == 0:
                    return
                first = isinstance(i, int) and i == 0
                if first and b:
                    pe.wait_ge(added, b * TPB)
                project_down(m - 1, 1 - s, first=first)

            def after(b):
                project_down((b + 1) * MT - 1, 1, last=True)
            over_steps(pe, body, first=1, after=after)


def build(nc, x, wmod, c, wjobs, sjobs, ffn, cos, sin, ident_dram, masks_dram, r_scratch, out):
    ctx = ExitStack()
    with ctx:
        al = Allocator(nc, ctx)
        hT_hi, hT_lo = al.sbuf("hT_hi", [P, KT, S], F32R), al.sbuf("hT_lo", [P, KT, S], F32R)
        acc = al.sbuf("acc", [P, ST, H])
        ident = al.sbuf("ident", [P, P])
        masks = al.sbuf("masks", [P, 2, P], BF16)
        mod_cols = al.sbuf("mod_cols", [P, 4 * KT])
        (pT_hi, x_place), pT_lo = al.sbuf_shared("pT_hi", [P, ST, QB]), al.sbuf("pT_lo", [P, ST, QB], F32R)
        x_again = [al.sem(f"x_again{b}") for b in range(NB)]
        attention_phase(nc, hT_hi, hT_lo, acc, ident, masks, pT_hi, pT_lo, x_place, mod_cols, x_again, x, wmod, c,
                        wjobs, sjobs, cos, sin, ident_dram, masks_dram, r_scratch)
        gates = al.sbuf("gates", [P, 2, H])
        raw = al.sbuf("raw", [P, 2, 3 * H], F16)
        raw_loaded = [al.sem("raw_loaded0"), al.sem("raw_loaded1")]
        residual_phase(nc, acc, x_place, x_again, mod_cols, gates, ident, hT_hi, hT_lo,
                       raw, raw_loaded, ffn)
        ffn_phase(nc, hT_hi, hT_lo, acc, gates[:, 1, :], raw, raw_loaded, ffn, out)


def kernel(L0_attn_hidden_states, L0_attn_scales_q, L0_attn_scales_k, L0_attn_scales_v, L0_attn_scales_o,
           L0_attn_qw_q, L0_attn_qw_k, L0_attn_qw_v, L0_attn_qw_o, L0_ffn_W_gate, L0_ffn_W_up, L0_ffn_W_down,
           L0_c, L0_wmod):
    import numpy as np
    import concourse.bacc as bacc
    from concourse.bass_utils import run_bass_kernel_spmd

    def by_head(w, heads):
        return w.reshape(-1, P, heads, HD).transpose(2, 1, 0, 3).reshape(heads, P, -1)

    def scale_by_head(s, heads):
        return s.reshape(KT, heads, HD).transpose(1, 0, 2).reshape(heads, H)

    def jobs(k, v, q, o):
        return np.ascontiguousarray(np.concatenate(
            [k[:, None], v[:, None], q.reshape(NKV, HPG, *q.shape[1:]), o.reshape(NKV, HPG, *o.shape[1:])], axis=1))

    def array(a):
        return np.asarray(a)

    wjobs = jobs(by_head(array(L0_attn_qw_k), NKV), by_head(array(L0_attn_qw_v), NKV),
                 by_head(array(L0_attn_qw_q), NH), array(L0_attn_qw_o).reshape(NH, HD, H))
    sjobs = jobs(scale_by_head(array(L0_attn_scales_k), NKV), scale_by_head(array(L0_attn_scales_v), NKV),
                 scale_by_head(array(L0_attn_scales_q), NH), array(L0_attn_scales_o))

    def ffn_side(w):
        return w.reshape(MT, P, KT, P).transpose(0, 3, 2, 1).reshape(MT, P, H)

    ffn = np.ascontiguousarray(np.concatenate(
        [ffn_side(array(L0_ffn_W_gate)), ffn_side(array(L0_ffn_W_up)),
         array(L0_ffn_W_down).T.reshape(MT, P, H)], axis=2))

    inv_freq = np.float32(1.0) / (10000.0 ** (np.arange(0, HD, 2) / HD)).astype(np.float32)
    angle = (np.arange(S, dtype=np.float32)[:, None] * inv_freq).astype(np.float64)
    cos = np.ascontiguousarray(np.concatenate([np.cos(angle), np.cos(angle)], axis=1).T.astype(np.float32))
    sin = np.ascontiguousarray(np.concatenate([-np.sin(angle), np.sin(angle)], axis=1).T.astype(np.float32))
    bf16 = mybir.dt.np(BF16)
    masks = np.zeros((P, 2, P), bf16)
    masks[:, 0] = np.eye(P)
    masks[:, 1] = np.triu(np.full((P, P), 1e37), 1)

    arrays = {"x": array(L0_attn_hidden_states)[0], "wmod": array(L0_wmod), "c": np.ascontiguousarray(array(L0_c).reshape(KT, P).T), "wjobs": wjobs,
              "sjobs": sjobs, "ffn": ffn, "cos": cos, "sin": sin, "ident": np.eye(P, dtype=np.float32), "masks": masks}
    nc = bacc.Bacc("TRN2", target_bir_lowering=False, num_devices=1)
    aps = {n: nc.dram_tensor("in_" + n, a.shape, mybir.dt.from_np(a.dtype), kind="ExternalInput").ap()
           for n, a in arrays.items()}
    r_scratch = nc.dram_tensor("r_scratch", (2, QB), F32, kind="Internal").ap()
    out = nc.dram_tensor("out", (S, H), F32, kind="ExternalOutput").ap()
    build(nc, aps["x"], aps["wmod"], aps["c"], aps["wjobs"], aps["sjobs"], aps["ffn"], aps["cos"], aps["sin"],
          aps["ident"], aps["masks"], r_scratch, out)
    r = run_bass_kernel_spmd(nc, [{"in_" + n: a for n, a in arrays.items()}], core_ids=[0])
    return r.results[0]["out"].reshape(1, S, H)
```
